# Optimizing a Trainium2 kernel written in Bass

```python
import numpy as np
import jax
import jax.numpy as jnp

def _softmax(x, axis=-1):
    return jax.nn.softmax(x, axis=axis)

def _gelu(x):
    return jax.nn.gelu(x, approximate=True)

def _silu(x):
    return jax.nn.silu(x)

def _sigmoid(x):
    return jax.nn.sigmoid(x)

def _layernorm(x, axis=-1, eps=1e-05):
    m = jnp.mean(x, axis=axis, keepdims=True)
    v = jnp.var(x, axis=axis, keepdims=True)
    return (x - m) / jnp.sqrt(v + eps)

def _scatter_add(tgt, idx, src, axis=0):
    return tgt.at[idx].add(src)

def _segment_sum(src, seg, n):
    return jax.ops.segment_sum(src, seg, n)
kernel_name = 'mk_flamingo_gated_d1_seqx_r8_eac5cc'

def setup_inputs(seed: int=0):
    np.random.seed(seed)
    _w = jnp.asarray

    def _rec_inputs():
        import jax
        import jax.numpy as jnp
        _rk = jax.random.key(seed)
        x = -4.161e-06 + 1 * jax.random.normal(jax.random.fold_in(_rk, 1), (16, 64, 256), jnp.float32)
        _lenS = 64 - jax.random.randint(jax.random.fold_in(_rk, 7), (16,), 0, max(1, 64 // 4) + 1, jnp.int32)
        _lenS2 = 64 - jax.random.randint(jax.random.fold_in(_rk, 8), (16,), 0, max(1, 64 // 4) + 1, jnp.int32)
        _ctx_2048P = jax.random.normal(jax.random.fold_in(_rk, 11), (16, 16, 256), jnp.float32)
        _ctx_2048c = jax.random.dirichlet(jax.random.fold_in(_rk, 511), 0.3 * jnp.ones((16,), jnp.float32), (16, 64))
        _ctx_2048t = jnp.einsum('bsk,bkd->bsd', _ctx_2048c, _ctx_2048P)
        _ctx_2048t = _ctx_2048t * jax.lax.rsqrt(jnp.mean(jnp.square(_ctx_2048t)) + 1e-12) * 0.953939
        ctx_2048 = -0.000192764 + 0.999654 * (_ctx_2048t + 0.3 * jax.random.normal(jax.random.fold_in(_rk, 611), (16, 64, 256), jnp.float32))
        _g = jax.random.normal(jax.random.fold_in(_rk, 9001), (2, 1), jnp.float32)
        _g = jnp.sign(_g) * jnp.maximum(jnp.abs(_g), 1.0) + (_g == 0) * 1.0
        g_xattn = _g[0]
        g_ffn = _g[1]
        return (x, ctx_2048, g_xattn, g_ffn)
    x, ctx_2048, g_xattn, g_ffn = _rec_inputs()

    def _L0_xattn_setup():
        import jax, jax.numpy as jnp
        import numpy as np
        FP8_MAX = 448.0
        EPS = 1e-05

        def _fp8_roundtrip(x):
            return x.astype(jnp.float8_e4m3fn).astype(jnp.float32)

        def _div_clamp_fp8(x, scale):
            y = jnp.clip(x.astype(jnp.float32) / scale, -FP8_MAX, FP8_MAX)
            y = y.astype(jnp.bfloat16).astype(jnp.float32)
            return _fp8_roundtrip(y)

        def _ln(x, w, b):
            mu = jnp.mean(x, axis=-1, keepdims=True)
            var = jnp.mean(jnp.square(x - mu), axis=-1, keepdims=True)
            return (x - mu) * jax.lax.rsqrt(var + EPS) * w + b

        def _fp8_linear_pertensor(x, wq, w_scale, in_scale):
            xq = _div_clamp_fp8(x, in_scale)
            return jnp.einsum('bsi,oi->bso', xq * in_scale, wq) * w_scale

        def _gqa(q, k, v):
            scale = 1.0 / np.sqrt(q.shape[-1])
            scores = jnp.einsum('bsghd,btgd->bghst', q, k) * scale
            p = jax.nn.softmax(scores, axis=-1)
            return jnp.einsum('bghst,btgd->bsghd', p, v)
        key = jax.random.key(seed)
        ks = jax.random.split(key, 8)
        B, S, SC, H, NH, G, D = (2, 256, 64, 256, 16, 8, 128)

        def qw(k, out_f, in_f):
            w = jax.random.normal(k, (out_f, in_f), jnp.float32) * 0.02
            sc = jnp.max(jnp.abs(w)) / FP8_MAX
            return (_fp8_roundtrip(w / sc), sc.astype(jnp.float32))
        wq, wq_s = qw(ks[0], NH * D, H)
        wqx, wqx_s = qw(ks[1], NH * D, H)
        wk, wk_s = qw(ks[2], G * D, H)
        wv, wv_s = qw(ks[3], G * D, H)
        wproj, wp_s = qw(ks[4], H, 2 * NH * D)
        return {'hidden_states': jax.random.normal(ks[5], (B, S, H), jnp.float32), 'cond': jax.random.normal(ks[6], (B, SC, H), jnp.float32), 'ln_w': jnp.ones((H,), jnp.float32), 'ln_b': jnp.zeros((H,), jnp.float32), 'wq': wq, 'wq_scale': wq_s, 'q_in_scale': jnp.full((H,), 0.05, jnp.float32), 'wqx': wqx, 'wqx_scale': wqx_s, 'qx_in_scale': jnp.full((H,), 0.05, jnp.float32), 'wk': wk, 'wk_scale': wk_s, 'k_in_scale': jnp.full((H,), 0.05, jnp.float32), 'wv': wv, 'wv_scale': wv_s, 'v_in_scale': jnp.full((H,), 0.05, jnp.float32), 'w_kv_x': jax.random.normal(ks[7], (2 * G * D, H), jnp.float32) * 0.02, 'qln_w': jnp.ones((D,), jnp.float32), 'qln_b': jnp.zeros((D,), jnp.float32), 'kln_w': jnp.ones((D,), jnp.float32), 'kln_b': jnp.zeros((D,), jnp.float32), 'qxln_w': jnp.ones((D,), jnp.float32), 'qxln_b': jnp.zeros((D,), jnp.float32), 'kxln_w': jnp.ones((D,), jnp.float32), 'kxln_b': jnp.zeros((D,), jnp.float32), 'wproj': wproj, 'proj_w_scale': wp_s, 'proj_in_scale': jnp.asarray(0.05, jnp.float32), 'proj_smooth': jnp.full((2 * NH * D,), 0.05, jnp.float32)}
    _L0_xattn_all = _L0_xattn_setup()
    _L0_xattn_in = {k: v for k, v in _L0_xattn_all.items() if k in ('ln_w', 'ln_b', 'wq', 'wq_scale', 'q_in_scale', 'wqx', 'wqx_scale', 'qx_in_scale', 'wk', 'wk_scale', 'k_in_scale', 'wv', 'wv_scale', 'v_in_scale', 'w_kv_x', 'qln_w', 'qln_b', 'kln_w', 'kln_b', 'qxln_w', 'qxln_b', 'kxln_w', 'kxln_b', 'wproj', 'proj_w_scale', 'proj_in_scale', 'proj_smooth')}
    del _L0_xattn_all

    def _L0_ffn_setup():
        import jax, jax.numpy as jnp
        import numpy as np
        DIM = 256
        EXPERT_DIM = 128
        N_EXPERTS = 16
        TOPK = 2
        N_SHARED = 1
        B, T = (4, 256)
        key = jax.random.key(seed)
        ks = jax.random.split(key, 9)
        s = 0.02
        return {'x': jax.random.normal(ks[0], (B, T, DIM), jnp.float32), 'router_w': jax.random.normal(ks[1], (N_EXPERTS, DIM), jnp.float32) * s, 'router_bias': jnp.zeros((N_EXPERTS,), jnp.float32), 'Wu': jax.random.normal(ks[2], (N_EXPERTS, DIM, EXPERT_DIM), jnp.float32) * s, 'Wg': jax.random.normal(ks[3], (N_EXPERTS, DIM, EXPERT_DIM), jnp.float32) * s, 'Wd': jax.random.normal(ks[4], (N_EXPERTS, EXPERT_DIM, DIM), jnp.float32) * s, 'Su': jax.random.normal(ks[5], (N_SHARED, DIM, EXPERT_DIM * TOPK), jnp.float32) * s, 'Sg': jax.random.normal(ks[6], (N_SHARED, DIM, EXPERT_DIM * TOPK), jnp.float32) * s, 'Sd': jax.random.normal(ks[7], (N_SHARED, EXPERT_DIM * TOPK, DIM), jnp.float32) * s}
    _L0_ffn_all = _L0_ffn_setup()
    _L0_ffn_in = {k: v for k, v in _L0_ffn_all.items() if k in ('router_w', 'router_bias', 'Wu', 'Wg', 'Wd', 'Su', 'Sg', 'Sd')}
    del _L0_ffn_all
    return {'x': x, 'ctx_2048': ctx_2048, 'g_xattn': g_xattn, 'g_ffn': g_ffn, 'L0_xattn_ln_w': _L0_xattn_in['ln_w'], 'L0_xattn_ln_b': _L0_xattn_in['ln_b'], 'L0_xattn_wq': _L0_xattn_in['wq'], 'L0_xattn_wq_scale': _L0_xattn_in['wq_scale'], 'L0_xattn_q_in_scale': _L0_xattn_in['q_in_scale'], 'L0_xattn_wqx': _L0_xattn_in['wqx'], 'L0_xattn_wqx_scale': _L0_xattn_in['wqx_scale'], 'L0_xattn_qx_in_scale': _L0_xattn_in['qx_in_scale'], 'L0_xattn_wk': _L0_xattn_in['wk'], 'L0_xattn_wk_scale': _L0_xattn_in['wk_scale'], 'L0_xattn_k_in_scale': _L0_xattn_in['k_in_scale'], 'L0_xattn_wv': _L0_xattn_in['wv'], 'L0_xattn_wv_scale': _L0_xattn_in['wv_scale'], 'L0_xattn_v_in_scale': _L0_xattn_in['v_in_scale'], 'L0_xattn_w_kv_x': _L0_xattn_in['w_kv_x'], 'L0_xattn_qln_w': _L0_xattn_in['qln_w'], 'L0_xattn_qln_b': _L0_xattn_in['qln_b'], 'L0_xattn_kln_w': _L0_xattn_in['kln_w'], 'L0_xattn_kln_b': _L0_xattn_in['kln_b'], 'L0_xattn_qxln_w': _L0_xattn_in['qxln_w'], 'L0_xattn_qxln_b': _L0_xattn_in['qxln_b'], 'L0_xattn_kxln_w': _L0_xattn_in['kxln_w'], 'L0_xattn_kxln_b': _L0_xattn_in['kxln_b'], 'L0_xattn_wproj': _L0_xattn_in['wproj'], 'L0_xattn_proj_w_scale': _L0_xattn_in['proj_w_scale'], 'L0_xattn_proj_in_scale': _L0_xattn_in['proj_in_scale'], 'L0_xattn_proj_smooth': _L0_xattn_in['proj_smooth'], 'L0_ffn_router_w': _L0_ffn_in['router_w'], 'L0_ffn_router_bias': _L0_ffn_in['router_bias'], 'L0_ffn_Wu': _L0_ffn_in['Wu'], 'L0_ffn_Wg': _L0_ffn_in['Wg'], 'L0_ffn_Wd': _L0_ffn_in['Wd'], 'L0_ffn_Su': _L0_ffn_in['Su'], 'L0_ffn_Sg': _L0_ffn_in['Sg'], 'L0_ffn_Sd': _L0_ffn_in['Sd']}

def reference(x, ctx_2048, g_xattn, g_ffn, L0_xattn_ln_w, L0_xattn_ln_b, L0_xattn_wq, L0_xattn_wq_scale, L0_xattn_q_in_scale, L0_xattn_wqx, L0_xattn_wqx_scale, L0_xattn_qx_in_scale, L0_xattn_wk, L0_xattn_wk_scale, L0_xattn_k_in_scale, L0_xattn_wv, L0_xattn_wv_scale, L0_xattn_v_in_scale, L0_xattn_w_kv_x, L0_xattn_qln_w, L0_xattn_qln_b, L0_xattn_kln_w, L0_xattn_kln_b, L0_xattn_qxln_w, L0_xattn_qxln_b, L0_xattn_kxln_w, L0_xattn_kxln_b, L0_xattn_wproj, L0_xattn_proj_w_scale, L0_xattn_proj_in_scale, L0_xattn_proj_smooth, L0_ffn_router_w, L0_ffn_router_bias, L0_ffn_Wu, L0_ffn_Wg, L0_ffn_Wd, L0_ffn_Su, L0_ffn_Sg, L0_ffn_Sd):
    import jax
    import jax.numpy as jnp

    def _L0_xattn_ref(hidden_states, cond, ln_w, ln_b, wq, wq_scale, q_in_scale, wqx, wqx_scale, qx_in_scale, wk, wk_scale, k_in_scale, wv, wv_scale, v_in_scale, w_kv_x, qln_w, qln_b, kln_w, kln_b, qxln_w, qxln_b, kxln_w, kxln_b, wproj, proj_w_scale, proj_in_scale, proj_smooth):
        import jax, jax.numpy as jnp
        import numpy as np
        FP8_MAX = 448.0
        EPS = 1e-05

        def _fp8_roundtrip(x):
            return x.astype(jnp.float8_e4m3fn).astype(jnp.float32)

        def _div_clamp_fp8(x, scale):
            y = jnp.clip(x.astype(jnp.float32) / scale, -FP8_MAX, FP8_MAX)
            y = y.astype(jnp.bfloat16).astype(jnp.float32)
            return _fp8_roundtrip(y)

        def _ln(x, w, b):
            mu = jnp.mean(x, axis=-1, keepdims=True)
            var = jnp.mean(jnp.square(x - mu), axis=-1, keepdims=True)
            return (x - mu) * jax.lax.rsqrt(var + EPS) * w + b

        def _fp8_linear_pertensor(x, wq, w_scale, in_scale):
            xq = _div_clamp_fp8(x, in_scale)
            return jnp.einsum('bsi,oi->bso', xq * in_scale, wq) * w_scale

        def _gqa(q, k, v):
            scale = 1.0 / np.sqrt(q.shape[-1])
            scores = jnp.einsum('bsghd,btgd->bghst', q, k) * scale
            p = jax.nn.softmax(scores, axis=-1)
            return jnp.einsum('bghst,btgd->bsghd', p, v)
        b, s, _ = hidden_states.shape
        sc = cond.shape[1]
        d = qln_w.shape[0]
        nh = wq.shape[0] // d
        g = wk.shape[0] // d
        hpg = nh // g
        ln_out = _ln(hidden_states, ln_w, ln_b)
        q = _fp8_linear_pertensor(ln_out, wq, wq_scale, q_in_scale).reshape(b, s, g, hpg, d)
        q = _ln(q, qln_w, qln_b)
        k = _fp8_linear_pertensor(ln_out, wk, wk_scale, k_in_scale).reshape(b, s, g, d)
        k = _ln(k, kln_w, kln_b)
        v = _fp8_linear_pertensor(ln_out, wv, wv_scale, v_in_scale).reshape(b, s, g, d)
        core = _gqa(q, k, v).reshape(b, s, nh * d)
        qx = _fp8_linear_pertensor(ln_out, wqx, wqx_scale, qx_in_scale).reshape(b, s, g, hpg, d)
        qx = _ln(qx, qxln_w, qxln_b)
        kvx = jnp.einsum('bsi,oi->bso', cond, w_kv_x)
        kx, vx = jnp.split(kvx, 2, axis=-1)
        kx = _ln(kx.reshape(b, sc, g, d), kxln_w, kxln_b)
        vx = vx.reshape(b, sc, g, d)
        xout = _gqa(qx, kx, vx).reshape(b, s, nh * d)
        cat = jnp.concatenate([core, xout], axis=-1)
        catq = _div_clamp_fp8(cat, proj_smooth)
        return jnp.einsum('bsi,oi->bso', catq, wproj) * (proj_in_scale * proj_w_scale)

    def _L0_ffn_ref(x, router_w, router_bias, Wu, Wg, Wd, Su, Sg, Sd):
        import jax, jax.numpy as jnp
        import numpy as np
        DIM = 256
        EXPERT_DIM = 128
        N_EXPERTS = 16
        TOPK = 2
        N_SHARED = 1
        B, T = (4, 256)
        Bx, Tx, D = x.shape
        flat = x.reshape(Bx * Tx, D)
        logits = flat @ router_w.T
        scores = jax.nn.softmax(logits, axis=-1)
        _, topk_idx = jax.lax.top_k(logits + router_bias, TOPK)
        topk_scores = jnp.take_along_axis(scores, topk_idx, axis=-1)
        topk_scores = topk_scores / topk_scores.sum(-1, keepdims=True)
        combine = jnp.einsum('nk,nke->ne', topk_scores, jax.nn.one_hot(topk_idx, N_EXPERTS, dtype=scores.dtype))
        out = jnp.zeros_like(flat)
        for e in range(N_EXPERTS):
            h = jax.nn.silu(flat @ Wu[e]) * (flat @ Wg[e])
            out = out + combine[:, e:e + 1] * (h @ Wd[e])
        for s in range(N_SHARED):
            out = out + jax.nn.silu(flat @ Su[s]) * (flat @ Sg[s]) @ Sd[s]
        return out.reshape(Bx, Tx, D)
    x = x + jnp.tanh(g_xattn[0]) * _L0_xattn_ref(_layernorm(x, axis=-1), ctx_2048, L0_xattn_ln_w, L0_xattn_ln_b, L0_xattn_wq, L0_xattn_wq_scale, L0_xattn_q_in_scale, L0_xattn_wqx, L0_xattn_wqx_scale, L0_xattn_qx_in_scale, L0_xattn_wk, L0_xattn_wk_scale, L0_xattn_k_in_scale, L0_xattn_wv, L0_xattn_wv_scale, L0_xattn_v_in_scale, L0_xattn_w_kv_x, L0_xattn_qln_w, L0_xattn_qln_b, L0_xattn_kln_w, L0_xattn_kln_b, L0_xattn_qxln_w, L0_xattn_qxln_b, L0_xattn_kxln_w, L0_xattn_kxln_b, L0_xattn_wproj, L0_xattn_proj_w_scale, L0_xattn_proj_in_scale, L0_xattn_proj_smooth)
    x = x + jnp.tanh(g_ffn[0]) * _L0_ffn_ref(_layernorm(x, axis=-1), L0_ffn_router_w, L0_ffn_router_bias, L0_ffn_Wu, L0_ffn_Wg, L0_ffn_Wd, L0_ffn_Su, L0_ffn_Sg, L0_ffn_Sd)
    return x

_drawn_inputs = setup_inputs


def setup_inputs(seed=0):
    import zlib

    import numpy as np

    out = dict(_drawn_inputs(seed))
    spreads = {'L0_xattn_ln_w': (1.0, 0.6),
     'L0_xattn_ln_b': (0.0, 0.319),
     'L0_xattn_q_in_scale': (0.05000000074505806, 0.6),
     'L0_xattn_qx_in_scale': (0.05000000074505806, 0.6),
     'L0_xattn_k_in_scale': (0.05000000074505806, 0.6),
     'L0_xattn_v_in_scale': (0.05000000074505806, 0.6),
     'L0_xattn_qln_w': (1.0, 0.6),
     'L0_xattn_qln_b': (0.0, 0.8),
     'L0_xattn_kln_w': (1.0, 0.6),
     'L0_xattn_kln_b': (0.0, 0.8),
     'L0_xattn_qxln_w': (1.0, 0.6),
     'L0_xattn_qxln_b': (0.0, 0.8),
     'L0_xattn_kxln_w': (1.0, 0.6),
     'L0_xattn_kxln_b': (0.0, 0.8),
     'L0_xattn_proj_smooth': (0.05000000074505806, 0.559),
     'L0_ffn_router_bias': (0.0, 0.8)}
    factors = {'L0_ffn_router_w': 7.644,
     'L0_ffn_Wu': 7.144,
     'L0_ffn_Wg': 7.051,
     'L0_ffn_Wd': 7.026,
     'L0_ffn_Su': 3.617,
     'L0_ffn_Sg': 3.564,
     'L0_ffn_Sd': 3.567}
    for name, (base, spread) in spreads.items():
        noise = np.random.default_rng([zlib.crc32(name.encode()), seed]).standard_normal(out[name].shape)
        drawn = base * np.exp(spread * noise) if base else spread * noise
        out[name] = jnp.asarray(drawn.astype(out[name].dtype))
    for name, factor in factors.items():
        out[name] = (out[name] * factor).astype(out[name].dtype)
    return out
```

```python
from contextlib import ExitStack

import numpy as np

import concourse.bass as bass
from concourse import mybir

F32 = mybir.dt.float32
F16 = mybir.dt.float16
BF16 = mybir.dt.bfloat16
U16 = mybir.dt.uint16
U32 = mybir.dt.uint32
ALU = mybir.AluOpType
ACT = mybir.ActivationFunctionType
AX = mybir.AxisListType

P = 128
NB, S, H = 16, 64, 256
TOK = NB * S
NT = TOK // P
HC = H // P
D = 128
NH, G = 16, 8
NE, TOPK, FE = 16, 2, 128
NSH = 2
NX = NE + NSH
EPS = 1e-5
FP8_MAX = 448.0
SCORE_SCALE = 1.0 / float(np.sqrt(D))
WKV_SCALE = 64.0
WF_SCALE = 16.0
NROW = 3 * NE + 1

COL = {}
_n = 0
for _name, _w in (("lnw", HC), ("lnb", HC), ("in_k", HC), ("in_q", HC), ("in_v", HC), ("in_qx", HC),
                  ("qw", 1), ("kw", 1), ("qxw", 1), ("kxw", 1), ("qb", 1), ("kb", 1), ("qxb", 1), ("kxb", 1),
                  ("smooth", 2 * NH), ("s_q", 1), ("s_k", 1), ("s_qx", 1), ("s_v", 1),
                  ("s_proj", 1), ("s_pin", 1), ("g_x", 1), ("g_f", 1)):
    COL[_name] = (_n, _n + _w)
    _n += _w
NCOL = _n

BANKS = [("k", 0), ("q", 0), ("q", 1), ("v", 0),
         ("k", 1), ("q", 2), ("q", 3), ("v", 1),
         ("kx", 0), ("qx", 0), ("qx", 1), ("vx", 0),
         ("kx", 1), ("qx", 2), ("qx", 3), ("vx", 1)]
NBK = 16
NLN = 12
XORDER = ("k", "q", "v", "qx")
KIND_COL = {"q": 0, "k": 1, "qx": 2, "kx": 3}


def ge(eng, sem, value):
    if isinstance(value, int) and value <= 0:
        return
    eng.wait_ge(sem, value)


def build(nc, x, cols, rowc, ident, sel, ctxT, wkvT, wqT, wkT, wvT, wqxT, wpT, rwT, wffn, out):
    ctx = ExitStack()
    with ctx:
        def sb(name, shape, dt):
            return ctx.enter_context(nc.sbuf_tensor(name, shape, dt))

        def bank(name):
            return ctx.enter_context(nc.psum_tensor(name, [P, 512], F32))

        def sem(name):
            return ctx.enter_context(nc.semaphore(name))

        proj_ps = [bank("proj_ps0"), bank("proj_ps1")]
        headT_ps = bank("headT_ps")
        probT_ps = bank("probT_ps")
        score_ps = bank("score_ps")
        pv_ps = [bank("pv_ps0"), bank("pv_ps1")]
        out_ps = bank("out_ps")
        wide_ps = [score_ps, out_ps, pv_ps[0], pv_ps[1]]

        xs = sb("xs", [P, NT * H], F32)
        colv = sb("colv", [P, NCOL], F32)
        rowv = sb("rowv", [P, 2 * NE], F32)
        idf = sb("idf", [P, P], F32)
        XH = sb("XH", [P, 4, HC, TOK], F16)
        XL = sb("XL", [P, 4, HC, TOK], F16)
        ctxh = sb("ctxh", [P, HC, TOK], F16)
        ctxl = sb("ctxl", [P, HC, TOK], F16)
        wkvh = sb("wkvh", [P, HC, 2 * G * D], F16)
        wkvl = sb("wkvl", [P, HC, 2 * G * D], F16)
        wb = {"q": sb("wq_sb", [P, HC, NH * D], BF16), "k": sb("wk_sb", [P, HC, G * D], BF16),
              "v": sb("wv_sb", [P, HC, G * D], BF16), "qx": sb("wqx_sb", [P, HC, NH * D], BF16)}
        wp = sb("wp_sb", [P, 2 * NH, H], BF16)
        rot = sb("rot", [P, 6, 512], F32)
        raw = [rot[:, i, :] for i in range(3)]
        nrm = [rot[:, 3 + i, :] for i in range(3)]
        xn = rot[:, 0:4, :].rearrange("p a b -> p (a b)")
        qT = sb("qT", [P, 2, 2 * NH, P], F32)
        kT = sb("kT", [P, 2, 2 * G, P], F32)
        vt = sb("vt", [P, 2, 2 * G * D], F32)
        reg1 = sb("reg1", [P, 2048], F32)
        reg2 = sb("reg2", [P, 2048], F32)
        xT = reg1[:, :].rearrange("p (c t) -> p c t", c=HC)
        prob = [reg1[:, 512 * i:512 * i + 512] for i in range(2)]
        probn = [reg1[:, 1024 + 512 * i:1536 + 512 * i] for i in range(2)]
        ctx_st = reg2[:, :]
        probT = [reg2[:, 512 * i:512 * i + 512] for i in range(2)]
        catq = [reg2[:, 1024 + 512 * i:1536 + 512 * i].bitcast(BF16) for i in range(2)]
        wkv_st = qT[:, 1, :, :].rearrange("p a b -> p (a b)")
        yv = sb("yv", [P, 1024], BF16)
        ya = sb("ya", [P, 1024], BF16)
        ym = sb("ym", [P, 1024], F16)
        ys = sb("ys", [P, 1024], F16)
        mx = sb("mx", [P, 8], F32)
        sm = sb("sm", [P, 8], F32)
        rinv = sb("rinv", [P, 2, 8], F32)
        st = sb("st", [P, 3, 4, 6], F32)
        mean2 = sb("mean2", [P, 3, 4], F32)
        vw = sb("vw", [P, 6, 4], F32)
        va = sb("va", [P, 3, 4], F32)
        vl = sb("vl", [P, 3, 4], F32)
        r0 = sb("r0", [P, 3, 4], F32)
        nw = sb("nw", [P, 5, 4], F32)
        cw = sb("cw", [P, 3, 4], F32)
        cb = sb("cb", [P, 3, 4], F32)
        sinv = sb("sinv", [P, 4 * HC], F32)
        smi = sb("smi", [P, 2 * NH], F32)
        lnC = sb("lnC", [P, 6, 4], F32)
        lnW = sb("lnW", [P, 4], F32)
        th = sb("th", [P, 2], F32)
        gate = sb("gate", [P, 3], F32)
        tst = sb("tst", [P, NT, 6], F32)
        tmv = sb("tmv", [P, NT, 2], F32)
        tw = sb("tw", [P, 8, NT], F32)
        tn = sb("tn", [P, 2, NT], F32)

        XHf = XH[:, :, :, :].rearrange("p a c t -> p (a c t)")
        XLf = XL[:, :, :, :].rearrange("p a c t -> p (a c t)")
        zh = XHf[:, 0:2048].rearrange("p (c t) -> p c t", c=HC)
        zl = XHf[:, 2048:4096].rearrange("p (c t) -> p c t", c=HC)
        zT = XLf[:, 0:4096].bitcast(F32).rearrange("p (c t) -> p c t", c=HC)
        WE = 3 * H
        wst = [XLf[:, 4096 + 2 * WE * i:4096 + 2 * WE * (i + 1)].bitcast(F32) for i in range(2)]
        qTh = qT[:, :, :, :].rearrange("p a b c -> p (a b c)")
        weh = [qTh[:, 384 * i:384 * (i + 1)].bitcast(F16) for i in range(2)]
        wel = [qTh[:, 768 + 384 * i:768 + 384 * (i + 1)].bitcast(F16) for i in range(2)]
        hs = [qTh[:, 1536 + 512 * i:2048 + 512 * i] for i in range(2)]
        ht = [qTh[:, 2560 + 512 * i:3072 + 512 * i] for i in range(2)]
        hf = [qTh[:, 3584 + 512 * i:4096 + 512 * i] for i in range(2)]
        hh = [qTh[:, 4608 + 256 * i:4864 + 256 * i].bitcast(F16) for i in range(2)]
        hl = [qTh[:, 5120 + 256 * i:5376 + 256 * i].bitcast(F16) for i in range(2)]
        yo = [qTh[:, 5632 + 256 * i:5888 + 256 * i] for i in range(NT)]
        kTf = kT[:, :, :, :].rearrange("p a b c -> p (a b c)")
        sel_sb = kTf[0:NROW, 0:NX * P // 2].bitcast(BF16).rearrange("p (e m) -> p e m", e=NX)
        combT = kTf[0:NROW, 1152:1664].bitcast(BF16)
        idb = kTf[:, 1664:1728].bitcast(BF16)
        rws = kTf[:, 1728:1760].rearrange("p (c e) -> p c e", c=HC)
        NTE = NT * NE
        rt = [kTf[:, 1792 + NTE * i:1792 + NTE * (i + 1)].rearrange("p (t e) -> p t e", t=NT) for i in range(9)]
        m8 = kTf[:, 3072:3136].rearrange("p (t k) -> p t k", t=NT)
        i8 = kTf[:, 3136:3200].bitcast(U32).rearrange("p (t k) -> p t k", t=NT)
        i8f = kTf[:, 3200:3264].rearrange("p (t k) -> p t k", t=NT)
        rs8 = kTf[:, 3264:3288].rearrange("p (a t) -> p a t", a=3)
        cbt = kTf[:, 3328:3328 + NT * 32].bitcast(BF16).rearrange("p (t e) -> p t e", t=NT)

        def col(name, c=0):
            a = COL[name][0] + c
            return colv[:, a:a + 1]

        ld_x = sem("ld_x")
        ld_small = sem("ld_small")
        ld_ctx = sem("ld_ctx")
        ld_wkv = sem("ld_wkv")
        ld_w = {k: sem("ld_w" + k) for k in ("k", "q", "v", "qx")}
        ld_wp = sem("ld_wp")
        ld_tail = sem("ld_tail")
        prep_done = sem("prep_done")
        tanh_done = sem("tanh_done")
        ln_in = sem("ln_in")
        ln_mid = sem("ln_mid")
        ln_root = sem("ln_root")
        dchain = sem("dchain")
        xn_done = sem("xn_done")
        xT_done = sem("xT_done")
        xT_evac = sem("xT_evac")
        q0_done = sem("q0_done")
        hi0_done = sem("hi0_done")
        xs_ready = sem("xs_ready")
        ctx_hi = sem("ctx_hi")
        ctx_ready = sem("ctx_ready")
        wkv_hi = sem("wkv_hi")
        wkv_ready = sem("wkv_ready")
        proj_done = sem("proj_done")
        proj_evac = sem("proj_evac")
        bn_done = sem("bn_done")
        achain = sem("achain")
        hchain = sem("hchain")
        var_done = sem("var_done")
        log_done = sem("log_done")
        root_done = sem("root_done")
        nchain = sem("nchain")
        coef_done = sem("coef_done")
        norm_done = sem("norm_done")
        headT_done = sem("headT_done")
        headT_evac = sem("headT_evac")
        score_done = sem("score_done")
        max_done = sem("max_done")
        sub_done = sem("sub_done")
        exp_done = sem("exp_done")
        sum_done = sem("sum_done")
        rinv_done = sem("rinv_done")
        probn_done = sem("probn_done")
        probT_done = sem("probT_done")
        probT_evac = sem("probT_evac")
        pv_done = sem("pv_done")
        y_done = sem("y_done")
        clip_done = sem("clip_done")
        abs_done = sem("abs_done")
        mag_done = sem("mag_done")
        big_done = sem("big_done")
        catq_done = sem("catq_done")
        op_done = sem("op_done")
        res_done = sem("res_done")
        zl_done = sem("zl_done")
        logit_done = sem("logit_done")
        rexp_in = sem("rexp_in")
        rexp_done = sem("rexp_done")
        comb_done = sem("comb_done")
        combT_done = sem("combT_done")
        combT_evac = sem("combT_evac")
        idb_done = sem("idb_done")
        we_ld = [sem("we_ld0"), sem("we_ld1")]
        we_hi = sem("we_hi")
        we_lo = sem("we_lo")
        up_done = sem("up_done")
        silu_done = sem("silu_done")
        prod_done = sem("prod_done")
        hid_done = sem("hid_done")
        hid_hi = sem("hid_hi")
        hid_lo = sem("hid_lo")
        down_done = sem("down_done")
        y_ready = sem("y_ready")
        stored = sem("stored")

        NU = 4
        ups = [(proj_ps[0], headT_ps, score_ps), (proj_ps[1], probT_ps, out_ps)]
        block = ctx.enter_context(nc.Block())
        LN_IDX = {}
        for u, (kind, _) in enumerate(BANKS):
            if kind not in ("v", "vx"):
                LN_IDX[u] = len(LN_IDX)

        @block.sync
        def _(sp):
            sp.dma_start(xs[:, :].rearrange("p (t d) -> p t d", t=NT),
                         x.rearrange("(t p) d -> p t d", p=P)).then_inc(ld_x, 16)
            sp.dma_start(colv[:, :], cols).then_inc(ld_small, 16)
            sp.dma_start(rowv[:, :], rowc).then_inc(ld_small, 16)
            sp.dma_start(idf[:, :], ident).then_inc(ld_small, 16)
            sp.dma_start(ctx_st.rearrange("p (c t) -> p c t", c=HC),
                         ctxT.rearrange("(c p) t -> p c t", p=P)).then_inc(ld_ctx, 16)
            sp.dma_start(wkv_st.rearrange("p (c t) -> p c t", c=HC),
                         wkvT.rearrange("(c p) t -> p c t", p=P)).then_inc(ld_wkv, 16)
            sp.wait_ge(proj_done, NBK * NT)
            for n in range(2):
                sp.dma_start(wst[n], wffn[n, :, :]).then_inc(we_ld[n], 16)
            for half in range(2):
                def load(e, par, n):
                    sp.wait_ge(we_lo, n + 1)
                    sp.wait_ge(we_hi, n + 1)
                    sp.dma_start(wst[par], wffn[bass.ds(e, 1), :, :].rearrange("a p n -> p (a n)")
                                 if not isinstance(e, int) else wffn[e, :, :]).then_inc(we_ld[par], 16)
                with sp.Fori(0, NX // 2 - 1) as i:
                    load(2 * i + 2, 0, NX * half + 2 * i)
                    load(2 * i + 3, 1, NX * half + 2 * i + 1)
                if half == 0:
                    load(0, 0, NX - 2)
                    load(1, 1, NX - 1)
            for t in range(NT):
                sp.wait_ge(y_ready, t + 1)
                sp.dma_start(out[t * P:(t + 1) * P, :], yo[t]).then_inc(stored, 16)
            sp.wait_ge(stored, 16 * NT)

        @block.gpsimd
        def _(gp):
            for k, w in (("k", wkT), ("q", wqT), ("v", wvT), ("qx", wqxT)):
                gp.dma_start(wb[k][:, :, :], w.rearrange("(c p) o -> p c o", p=P)).then_inc(ld_w[k], 16)
            gp.dma_start(wp[:, :, :], wpT.rearrange("(h p) o -> p h o", p=P)).then_inc(ld_wp, 16)

            def chained(sem, ins, count):
                ins.then_inc(sem, 1)
                gp.wait_ge(sem, count)

            def variance(t, u):
                m = LN_IDX[u]
                s = m % 3
                kc = KIND_COL[BANKS[u][0]]
                n0 = 4 * (NLN * t + m)

                def const(i):
                    return lnC[:, i, kc:kc + 1].to_broadcast([P, 4])

                gp.wait_ge(bn_done, NLN * t + m + 1)
                if m >= 3 or not (isinstance(t, int) and t == 0):
                    gp.wait_ge(norm_done, NLN * t + m - 2)
                ge(gp, var_done, NLN * t + m)
                gp.tensor_tensor(mean2[:, s, :], st[:, s, :, 1], st[:, s, :, 4], ALU.add)
                gp.tensor_tensor(vw[:, 0, :], st[:, s, :, 2], st[:, s, :, 5], ALU.add)
                chained(achain, gp.tensor_tensor(vw[:, 1, :], st[:, s, :, 1], st[:, s, :, 4], ALU.subtract),
                        n0 + 1)
                chained(achain, gp.tensor_tensor(vw[:, 2, :], vw[:, 1, :], vw[:, 1, :], ALU.mult), n0 + 2)
                gp.tensor_tensor(vw[:, 3, :], vw[:, 0, :], const(0), ALU.mult)
                chained(achain, gp.tensor_tensor(vw[:, 4, :], vw[:, 2, :], const(1), ALU.mult), n0 + 3)
                chained(achain, gp.tensor_tensor(vw[:, 5, :], vw[:, 3, :], vw[:, 4, :], ALU.add), n0 + 4)
                gp.tensor_tensor(va[:, s, :], vw[:, 5, :], const(2), ALU.add).then_inc(var_done, 1)

            def coefficients(t, u):
                m = LN_IDX[u]
                s = m % 3
                kc = KIND_COL[BANKS[u][0]]
                n0 = 5 * (NLN * t + m)

                def const(i):
                    return lnC[:, i, kc:kc + 1].to_broadcast([P, 4])

                gp.wait_ge(root_done, NLN * t + m + 1)
                ge(gp, coef_done, NLN * t + m)
                chained(nchain, gp.tensor_tensor(nw[:, 0, :], va[:, s, :], r0[:, s, :], ALU.mult), n0 + 1)
                chained(nchain, gp.tensor_tensor(nw[:, 1, :], nw[:, 0, :], r0[:, s, :], ALU.mult), n0 + 2)
                chained(nchain, gp.tensor_tensor(nw[:, 2, :], nw[:, 1, :], const(3), ALU.mult), n0 + 3)
                chained(nchain, gp.tensor_tensor(nw[:, 3, :], nw[:, 2, :], const(4), ALU.add), n0 + 4)
                chained(nchain, gp.tensor_tensor(cw[:, s, :], nw[:, 3, :], r0[:, s, :], ALU.mult), n0 + 5)
                gp.tensor_tensor(nw[:, 0, :], mean2[:, s, :], lnC[:, 5, 0:1].to_broadcast([P, 4]), ALU.mult)\
                  .then_inc(hchain, 1)
                gp.wait_ge(hchain, NLN * t + m + 1)
                gp.tensor_tensor(cb[:, s, :], nw[:, 0, :], cw[:, s, :], ALU.mult).then_inc(coef_done, 1)

            def normalise(w, c):
                gp.wait_ge(rinv_done, w + 1)
                ge(gp, probT_done, w - 1)
                gp.tensor_tensor(probn[c % 2].rearrange("p (g t) -> p g t", t=S),
                                 prob[c % 2].rearrange("p (g t) -> p g t", t=S),
                                 rinv[:, c % 2, :].unsqueeze(2).to_broadcast([P, 8, S]),
                                 ALU.mult).then_inc(probn_done, 1)

            def step(tb, tc, c):
                if tb is not None:
                    variance(tb, 4 * c)
                    variance(tb, 4 * c + 1)
                    coefficients(tb, 4 * c)
                if tc is not None:
                    normalise(NU * tc + c, c)
                if tb is not None:
                    coefficients(tb, 4 * c + 1)
                    variance(tb, 4 * c + 2)
                    coefficients(tb, 4 * c + 2)

            for c in range(NU):
                step(0, None, c)
            for c in range(NU):
                step(1, 0, c)
            with gp.Fori(0, (NT - 2) // 2) as i:
                for d in range(2):
                    for c in range(NU):
                        step(2 * i + 2 + d, 2 * i + 1 + d, c)
            for c in range(NU):
                step(None, NT - 1, c)
            gp.wait_ge(score_done, NU * NT)
            gp.dma_start(kTf[0:NROW, 0:NX * P // 2].bitcast(BF16), sel).then_inc(ld_tail, 16)
            gp.dma_start(rws, rwT.rearrange("(c p) e -> p c e", p=P)).then_inc(ld_tail, 16)
            def low(n, par):
                gp.wait_ge(hid_hi, n + 1)
                ge(gp, down_done, n - 1)
                gp.tensor_tensor(hl[par], hf[par], hh[par], ALU.subtract).then_inc(hid_lo, 1)

            for half in range(2):
                if half == 0:
                    low(0, 0)
                    low(1, 1)
                    with gp.Fori(1, NX // 2) as i:
                        low(2 * i, 0)
                        low(2 * i + 1, 1)
                else:
                    with gp.Fori(0, NX // 2) as i:
                        low(NX + 2 * i, 0)
                        low(NX + 2 * i + 1, 1)

        @block.scalar
        def _(act):
            act.wait_ge(ld_small, 48)
            a = COL["g_x"][0]
            act.activation(th[:, :], colv[:, a:a + 2], ACT.Tanh).then_inc(tanh_done, 1)

            def root(n, src, mid, dst):
                act.wait_ge(ln_in, n + 1)
                act.activation(mid, src, ACT.Ln).then_inc(ln_mid, 1)
                act.wait_ge(ln_mid, n + 1)
                act.activation(dst, mid, ACT.Exp, scale=-0.5).then_inc(ln_root, 1)

            root(0, tw[:, 0, :], tw[:, 1, :], tw[:, 2, :])
            root(1, tw[:, 0, :], tw[:, 1, :], tw[:, 2, :])
            for k in range(4):
                c, half = k // 2, k % 2
                act.wait_ge(xT_done, k + 1)
                act.activation(xT[:, c, half * 512:half * 512 + 512], wide_ps[k][:, :], ACT.Identity,
                               scale=col("lnw", c), bias=col("lnb", c)).then_inc(xT_evac, 1)
            act.wait_ge(ld_ctx, 16)
            act.activation(ctxh[:, :, :].rearrange("p c t -> p (c t)"), ctx_st, ACT.Copy).then_inc(ctx_hi, 1)
            act.wait_ge(ld_wkv, 16)
            act.activation(wkvh[:, :, :].rearrange("p c t -> p (c t)"), wkv_st, ACT.Copy,
                           scale=WKV_SCALE).then_inc(wkv_hi, 1)
            for n in range(4 * HC):
                j, c = n // HC, n % HC
                act.wait_ge(q0_done, n + 1)
                act.activation(XH[:, j, c, :], XL[:, j, c, :].bitcast(BF16), ACT.Copy,
                               scale=col("in_" + XORDER[j], c)).then_inc(hi0_done, 1)

            def evacuate(t, u, par):
                kind, b = BANKS[u]
                n = NBK * t + u
                act.wait_ge(proj_done, n + 1)
                if kind in ("v", "vx"):
                    off = (G * D if kind == "vx" else 0) + 512 * b
                    if not (isinstance(t, int) and t < 2):
                        act.wait_ge(pv_done, NU * (t - 1))
                    scale = col("s_v") if kind == "v" else 1.0 / WKV_SCALE
                    act.activation(vt[:, par, off:off + 512], proj_ps[u % 2][:, :], ACT.Copy,
                                   scale=scale).then_inc(proj_evac, 1)
                else:
                    m = LN_IDX[u]
                    if m >= 3 or not (isinstance(t, int) and t == 0):
                        act.wait_ge(norm_done, NLN * t + m - 2)
                    act.activation(raw[m % 3], proj_ps[u % 2][:, :], ACT.Copy).then_inc(proj_evac, 1)

            def roots(t, u):
                m = LN_IDX[u]
                s = m % 3
                act.wait_ge(var_done, NLN * t + m + 1)
                if m >= 3 or not (isinstance(t, int) and t == 0):
                    act.wait_ge(coef_done, NLN * t + m - 2)
                act.activation(vl[:, s, :], va[:, s, :], ACT.Ln).then_inc(log_done, 1)
                act.wait_ge(log_done, NLN * t + m + 1)
                act.activation(r0[:, s, :], vl[:, s, :], ACT.Exp, scale=-0.5).then_inc(root_done, 1)

            def heads_out(t, u, par):
                kind, b = BANKS[u]
                m = LN_IDX[u]
                act.wait_ge(headT_done, NLN * t + m + 1)
                if not (isinstance(t, int) and t < 2):
                    act.wait_ge(score_done, NU * (t - 1))
                if kind in ("q", "qx"):
                    h0 = (NH if kind == "qx" else 0) + 4 * b
                    dst = qT[:, par, h0:h0 + 4, :]
                else:
                    g0 = (G if kind == "kx" else 0) + 4 * b
                    dst = kT[:, par, g0:g0 + 4, :]
                act.activation(dst, headT_ps[:, :].rearrange("p (h t) -> p h t", h=4), ACT.Identity,
                               scale=col(kind + "w"), bias=col(kind + "b")).then_inc(headT_evac, 1)

            def expo(w, c):
                act.wait_ge(sub_done, w + 1)
                act.activation(prob[c % 2], prob[c % 2], ACT.Exp, scale=SCORE_SCALE).then_inc(exp_done, 1)

            def prob_out(w, c):
                act.wait_ge(probT_done, w + 1)
                ge(act, pv_done, w - 1)
                act.activation(probT[c % 2], probT_ps[:, :], ACT.Copy).then_inc(probT_evac, 1)

            def step(tb, pb, tc, c):
                if tb is not None:
                    evacuate(tb, 4 * c, pb)
                    evacuate(tb, 4 * c + 1, pb)
                if tc is not None:
                    expo(NU * tc + c, c)
                if tb is not None:
                    roots(tb, 4 * c)
                    evacuate(tb, 4 * c + 2, pb)
                    roots(tb, 4 * c + 1)
                    evacuate(tb, 4 * c + 3, pb)
                    roots(tb, 4 * c + 2)
                if tc is not None:
                    prob_out(NU * tc + c, c)
                if tb is not None:
                    for u in range(4 * c, 4 * c + 3):
                        heads_out(tb, u, pb)

            for c in range(NU):
                step(0, 0, None, c)
            for c in range(NU):
                step(1, 1, 0, c)
            with act.Fori(0, (NT - 2) // 2) as i:
                for d in range(2):
                    for c in range(NU):
                        step(2 * i + 2 + d, d, 2 * i + 1 + d, c)
            for c in range(NU):
                step(None, None, NT - 1, c)
            root(2, tw[:, 0, :], tw[:, 1, :], tw[:, 2, :])
            for k in range(4):
                c, half = k // 2, k % 2
                act.wait_ge(xT_done, 4 + k + 1)
                src = wide_ps[k][:, :]
                act.activation(zh[:, c, half * 512:half * 512 + 512], src, ACT.Copy)
                act.activation(zT[:, c, half * 512:half * 512 + 512], src, ACT.Copy).then_inc(xT_evac, 1)
            act.wait_ge(rexp_in, 1)
            act.activation(rt[2], rt[2], ACT.Exp).then_inc(rexp_done, 1)

            def split_hi(n, par, k):
                act.wait_ge(we_ld[par], 16 * (k + 1))
                ge(act, down_done, n - 1)
                act.activation(weh[par], wst[par], ACT.Copy, scale=WF_SCALE).then_inc(we_hi, 1)

            def silu(n, par):
                act.wait_ge(up_done, n + 1)
                ge(act, prod_done, n - 1)
                act.activation(hs[par], ups[par][0][:, :], ACT.Silu, scale=1.0 / WF_SCALE)\
                   .then_inc(silu_done, 1)

            def hidden_hi(n, par):
                act.wait_ge(hid_done, n + 1)
                ge(act, down_done, n - 1)
                act.activation(hh[par], hf[par], ACT.Copy).then_inc(hid_hi, 1)

            split_hi(0, 0, 0)
            for half in range(2):
                def pair(n, k, last=False):
                    silu_after = n
                    split_hi(n + 1, 1, k)
                    silu(silu_after, 0)
                    hidden_hi(n, 0)
                    if not last:
                        split_hi(n + 2, 0, k + 1)
                    silu(n + 1, 1)
                    hidden_hi(n + 1, 1)
                base, kb = NX * half, NX // 2 * half
                if half == 0:
                    pair(0, 0)
                    with act.Fori(1, NX // 2) as i:
                        pair(2 * i, i)
                else:
                    with act.Fori(0, NX // 2 - 1) as i:
                        pair(base + 2 * i, i + kb)
                    pair(base + NX - 2, kb + NX // 2 - 1, last=True)

        @block.tensor
        def _(pe):
            def wide_transposes(n0, done):
                for k in range(4):
                    c, half = k // 2, k % 2
                    for j in range(4):
                        t = 4 * half + j
                        mm = pe.transpose(wide_ps[k][:, j * P:(j + 1) * P],
                                          xn[:, t * H + c * P:t * H + c * P + P], idf[:, :])
                    mm.then_inc(done, 1)

            pe.wait_ge(ld_small, 48)
            pe.wait_ge(xn_done, 1)
            wide_transposes(0, xT_done)

            def project(t, u, first):
                kind, b = BANKS[u]
                n = NBK * t + u
                ge(pe, proj_evac, n - 1)
                ps = proj_ps[u % 2][:, :]
                if kind in ("kx", "vx"):
                    if first:
                        pe.wait_ge(ctx_ready, 1)
                        pe.wait_ge(wkv_ready, 1)
                    o = (G * D if kind == "vx" else 0) + 512 * b
                    parts = [(ctxh, wkvh), (ctxh, wkvl), (ctxl, wkvh)]
                    k = 0
                    for a, w in parts:
                        for c in range(HC):
                            lhs = a[:, c, bass.ds(t * P, P)]
                            mm = pe.matmul(ps, lhs, w[:, c, o:o + 512], start=(k == 0), stop=(k == 5))
                            k += 1
                else:
                    j = XORDER.index(kind)
                    if first:
                        pe.wait_ge(xs_ready, HC * (j + 1))
                        pe.wait_ge(ld_w[kind], 16)
                    k = 0
                    for a in (XH, XL):
                        for c in range(HC):
                            lhs = a[:, j, c, bass.ds(t * P, P)]
                            mm = pe.matmul(ps, lhs, wb[kind][:, c, 512 * b:512 * b + 512],
                                           start=(k == 0), stop=(k == 3))
                            k += 1
                mm.then_inc(proj_done, 1)

            def head_transposes(t, u):
                m = LN_IDX[u]
                pe.wait_ge(norm_done, NLN * t + m + 1)
                ge(pe, headT_evac, NLN * t + m)
                for h in range(4):
                    if BANKS[u][0] in ("q", "qx"):
                        dst = headT_ps[:, :].rearrange("p (g b h s) -> p g b h s", g=2, b=2, h=2)[:, h // 2, :, h % 2, :]
                    else:
                        dst = headT_ps[:, h * P:(h + 1) * P]
                    mm = pe.transpose(dst, nrm[m % 3][:, h * D:(h + 1) * D],
                                      idf[:, :])
                mm.then_inc(headT_done, 1)

            def scores(t, c, par):
                w = NU * t + c
                cross, gh = c // 2, c % 2
                pe.wait_ge(headT_evac, NLN * (t + 1))
                ge(pe, sub_done, w)
                for gi in range(4):
                    g = 4 * gh + gi
                    for b in range(2):
                        q2 = qT[:, par, NH * cross + 2 * g + b, :]
                        mm = pe.matmul(score_ps[:, (2 * gi + b) * S:(2 * gi + b + 1) * S], q2,
                                       kT[:, par, G * cross + g, b * S:(b + 1) * S], start=True, stop=True)
                mm.then_inc(score_done, 1)

            def prob_transposes(w, c):
                pe.wait_ge(probn_done, w + 1)
                ge(pe, probT_evac, w)
                for gi in range(4):
                    mm = pe.transpose(probT_ps[:, gi * P:(gi + 1) * P], probn[c % 2][:, gi * P:(gi + 1) * P],
                                      idf[:, :])
                mm.then_inc(probT_done, 1)

            def values(t, c, par):
                w = NU * t + c
                cross, gh = c // 2, c % 2
                pe.wait_ge(probT_evac, w + 1)
                pe.wait_ge(proj_evac, NBK * (t + 1))
                ge(pe, y_done, w)
                for gi in range(4):
                    o = G * D * cross + (4 * gh + gi) * D
                    for b in range(2):
                        mm = pe.matmul(pv_ps[b][:, gi * P:(gi + 1) * P], vt[b * S:(b + 1) * S, par, o:o + D],
                                       probT[c % 2][b * S:(b + 1) * S, gi * P:(gi + 1) * P],
                                       start=True, stop=True)
                mm.then_inc(pv_done, 1)

            def output(t, c):
                w = NU * t + c
                pe.wait_ge(catq_done, w + 1)
                if c == 0:
                    ge(pe, res_done, t)
                for h in range(8):
                    hd = 8 * c + h
                    mm = pe.matmul(out_ps[:, 0:H], catq[c % 2][:, h * P:(h + 1) * P], wp[:, hd, :],
                                   start=(c == 0 and h == 0), stop=(c == NU - 1 and h == 7))
                mm.then_inc(op_done, 1)

            def step(tb, tc, par, c, first=False, prev=None):
                if tc is not None:
                    scores(tc, c, par)
                if tb is not None:
                    for u in range(4 * c, 4 * c + 3):
                        project(tb, u, first)
                if tc is not None:
                    prob_transposes(NU * tc + c, c)
                if tb is not None:
                    project(tb, 4 * c + 3, first)
                    head_transposes(tb, 4 * c)
                    head_transposes(tb, 4 * c + 1)
                if tc is not None:
                    values(tc, c, par)
                if tb is not None:
                    head_transposes(tb, 4 * c + 2)
                if c > 0 and tc is not None:
                    output(tc, c - 1)
                elif prev is not None:
                    output(prev, NU - 1)

            pe.wait_ge(xT_evac, 4)
            for c in range(NU):
                step(0, None, 0, c, first=True)
            pe.wait_ge(ld_wp, 16)
            for c in range(NU):
                step(1, 0, 0, c)
            with pe.Fori(0, (NT - 2) // 2) as i:
                for d in range(2):
                    for c in range(NU):
                        tc = 2 * i + 1 + d
                        step(tc + 1, tc, 1 - d, c, prev=(tc - 1) if c == 0 else None)
            for c in range(NU):
                step(None, NT - 1, 1, c, prev=NT - 2 if c == 0 else None)
            output(NT - 1, NU - 1)
            pe.wait_ge(xn_done, 2)
            wide_transposes(4, xT_done)
            pe.wait_ge(xT_evac, 8)
            pe.wait_ge(ld_tail, 32)
            for t in range(NT):
                for c in range(HC):
                    mm = pe.matmul(proj_ps[0][:, t * NE:(t + 1) * NE], zT[:, c, t * P:(t + 1) * P],
                                   rws[:, c, :], start=(c == 0), stop=(c == HC - 1))
            mm.then_inc(logit_done, 1)
            pe.wait_ge(comb_done, 1)
            cps = headT_ps[:, :].bitcast(BF16)
            for t in range(NT):
                mm = pe.transpose(cps[0:NROW, t * P:(t + 1) * P], cbt[:, t, 0:NROW], idb)
            mm.then_inc(combT_done, 1)

            pe.wait_ge(combT_evac, 1)
            pe.wait_ge(zl_done, 4)

            def up(n, e, par, half):
                pe.wait_ge(we_lo, n + 1)
                pe.wait_ge(we_hi, n + 1)
                ge(pe, hid_done, n - 1)
                for wo, ps in ((0, ups[par][0]), (H, ups[par][1])):
                    k = 0
                    for w, z in ((weh[par], zh), (wel[par], zh), (weh[par], zl)):
                        for c in range(HC):
                            pe.matmul(ps[:, :], w[:, wo + c * P:wo + c * P + P],
                                      z[:, c, half * 512:half * 512 + 512], start=(k == 0), stop=(k == 5))
                            k += 1
                pe.matmul(ups[par][2][:, :], sel_sb[:, e, :] if isinstance(e, int)
                          else sel_sb[:, bass.ds(e, 1), :].rearrange("p a m -> p (a m)"),
                          combT[:, half * 512:half * 512 + 512], start=True, stop=True).then_inc(up_done, 1)

            def down(n, par, first, last):
                pe.wait_ge(hid_lo, n + 1)
                for j in range(4):
                    ps = pv_ps[j // 2][:, (j % 2) * H:(j % 2) * H + H]
                    tj = slice(j * P, j * P + P)
                    for k, (a, w) in enumerate(((hh, weh), (hl, weh), (hh, wel))):
                        mm = pe.matmul(ps, a[par][:, tj], w[par][:, 2 * H:3 * H],
                                       start=(first and j % 2 == 0 and k == 0), stop=(last and k == 2),
                                       skip_group_check=True)
                mm.then_inc(down_done, 1)

            for half in range(2):
                base = NX * half
                up(base, 0, 0, half)
                if half == 1:
                    pe.wait_ge(y_ready, 4)
                up(base + 1, 1, 1, half)
                down(base, 0, True, False)
                up(base + 2, 2, 0, half)
                down(base + 1, 1, False, False)
                with pe.Fori(1, NX // 2 - 1) as i:
                    up(base + 2 * i + 1, 2 * i + 1, 1, half)
                    down(base + 2 * i, 0, False, False)
                    up(base + 2 * i + 2, 2 * i + 2, 0, half)
                    down(base + 2 * i + 1, 1, False, False)
                up(base + NX - 1, NX - 1, 1, half)
                down(base + NX - 2, 0, False, False)
                down(base + NX - 1, 1, False, True)

        @block.vector
        def _(ve):
            links = [0]

            def link(ins):
                links[0] += 1
                ins.then_inc(dchain, 1)
                ve.wait_ge(dchain, links[0])

            def newton(r, v, a, b):
                link(ve.tensor_tensor(a, v, r, ALU.mult))
                link(ve.tensor_tensor(b, a, r, ALU.mult))
                link(ve.tensor_scalar(a, b, -0.5, 1.5, ALU.mult, ALU.add))
                link(ve.tensor_tensor(r, r, a, ALU.mult))

            def row_stats():
                for t in range(NT):
                    ins = ve.bn_stats(tst[:, t, :], xs[:, t * H:(t + 1) * H])
                link(ins)
                for t in range(NT):
                    ins = ve.bn_aggr(tmv[:, t, :], tst[:, t, :])
                link(ins)

            ve.wait_ge(ld_small, 48)
            a0, b0 = COL["in_k"][0], COL["in_qx"][1]
            ve.reciprocal(sinv[:, :], colv[:, a0:b0])
            a0, b0 = COL["smooth"]
            ve.reciprocal(smi[:, :], colv[:, a0:b0])
            ve.memset(lnW[:, 3:4], 1.0 / WKV_SCALE)
            a0 = COL["s_q"][0]
            link(ve.tensor_copy(lnW[:, 0:3], colv[:, a0:a0 + 3]))
            ve.memset(lnC[:, 2, :], EPS)
            ve.memset(lnC[:, 5, :], 0.5)
            link(ve.tensor_scalar(lnC[:, 0, :], lnW[:, :], 1.0 / D, None, ALU.mult))
            link(ve.tensor_tensor(lnC[:, 0, :], lnC[:, 0, :], lnW[:, :], ALU.mult))
            ve.tensor_scalar(lnC[:, 1, :], lnC[:, 0, :], D / 4.0, None, ALU.mult)
            ve.tensor_scalar(lnC[:, 3, :], lnW[:, :], -0.5, None, ALU.mult)
            link(ve.tensor_scalar(lnC[:, 4, :], lnW[:, :], 1.5, None, ALU.mult))
            ve.wait_ge(tanh_done, 1)
            ve.tensor_scalar(gate[:, 0:1], th[:, 0:1], col("s_proj"), None, ALU.mult)
            link(ve.tensor_scalar(gate[:, 1:2], th[:, 1:2], 1.0 / WF_SCALE, None, ALU.mult))
            link(ve.tensor_scalar(gate[:, 2:3], gate[:, 0:1], col("s_pin"), None, ALU.mult))

            ve.wait_ge(ld_x, 16)
            row_stats()
            var, mean = tmv[:, :, 1], tmv[:, :, 0]
            link(ve.tensor_scalar(tw[:, 0, :], var, EPS, None, ALU.add))
            ve.tensor_scalar(tw[:, 3, :], var, 1.0, None, ALU.mult).then_inc(ln_in, 1)
            ve.wait_ge(ln_root, 1)
            newton(tw[:, 2, :], tw[:, 0, :], tw[:, 4, :], tw[:, 5, :])
            link(ve.tensor_copy(tn[:, 0, :], tw[:, 2, :]))
            link(ve.tensor_tensor(tw[:, 4, :], tn[:, 0, :], tn[:, 0, :], ALU.mult))
            link(ve.tensor_tensor(tw[:, 5, :], tw[:, 4, :], var, ALU.mult))
            link(ve.tensor_scalar(tw[:, 0, :], tw[:, 5, :], EPS, None, ALU.add))
            ve.tensor_scalar(tw[:, 3, :], var, 1.0, None, ALU.mult).then_inc(ln_in, 1)
            ve.wait_ge(ln_root, 2)
            newton(tw[:, 2, :], tw[:, 0, :], tw[:, 4, :], tw[:, 5, :])
            link(ve.tensor_tensor(tn[:, 0, :], tn[:, 0, :], tw[:, 2, :], ALU.mult))
            link(ve.scalar_tensor_tensor(tn[:, 1, :], mean, -1.0, tn[:, 0, :], ALU.mult, ALU.mult))

            def row_norm():
                for t in range(NT):
                    ins = ve.tensor_scalar(xn[:, t * H:(t + 1) * H], xs[:, t * H:(t + 1) * H],
                                           tn[:, 0, t:t + 1], tn[:, 1, t:t + 1], ALU.mult, ALU.add)
                ins.then_inc(xn_done, 1)

            row_norm()

            def to_grid(q, wait_free, q_sem, n):
                ve.wait_ge(clip_done, n)
                ve.tensor_scalar(ya[:, :].bitcast(U16), yv[:, :].bitcast(U16), 0x7FFF, None,
                                 ALU.bitwise_and).then_inc(abs_done, 1)
                ve.wait_ge(abs_done, n)
                ve.tensor_scalar(ym[:, :], ya[:, :], 128.0, 3.0, ALU.mult, ALU.max).then_inc(mag_done, 1)
                ve.wait_ge(mag_done, n)
                ve.tensor_tensor(ys[:, :], yv[:, :], ym[:, :], ALU.add).then_inc(big_done, 1)
                ve.wait_ge(big_done, n)
                wait_free()
                ve.tensor_tensor(q, ys[:, :], ym[:, :], ALU.subtract).then_inc(q_sem, 1)

            def low0(n):
                j, c = n // HC, n % HC
                ve.wait_ge(hi0_done, n + 1)
                ve.scalar_tensor_tensor(XL[:, j, c, :], XL[:, j, c, :].bitcast(BF16),
                                        col("in_" + XORDER[j], c), XH[:, j, c, :],
                                        ALU.mult, ALU.subtract).then_inc(xs_ready, 1)

            for n in range(4 * HC):
                j, c = n // HC, n % HC
                ve.wait_ge(xT_evac, 2 * (c + 1))
                link(ve.tensor_scalar(yv[:, :], xT[:, c, :], sinv[:, n:n + 1], -FP8_MAX, ALU.mult, ALU.max))
                ve.tensor_scalar(yv[:, :], yv[:, :], FP8_MAX, None, ALU.min).then_inc(clip_done, 1)
                to_grid(XL[:, j, c, :].bitcast(BF16), lambda: None, q0_done, n + 1)
                if n > 0:
                    low0(n - 1)
            low0(4 * HC - 1)
            Q0 = 4 * HC
            ve.wait_ge(ctx_hi, 1)
            ve.tensor_tensor(ctxl[:, :, :].rearrange("p c t -> p (c t)"), ctx_st,
                             ctxh[:, :, :].rearrange("p c t -> p (c t)"), ALU.subtract).then_inc(ctx_ready, 1)
            ve.wait_ge(wkv_hi, 1)
            ve.scalar_tensor_tensor(wkvl[:, :, :].rearrange("p c t -> p (c t)"), wkv_st, WKV_SCALE,
                                    wkvh[:, :, :].rearrange("p c t -> p (c t)"),
                                    ALU.mult, ALU.subtract).then_inc(wkv_ready, 1)

            def stats(t, u):
                m = LN_IDX[u]
                s = m % 3
                ve.wait_ge(proj_evac, NBK * t + u + 1)
                for h in range(4):
                    ins = ve.bn_stats(st[:, s, h, :], raw[s][:, h * D:(h + 1) * D])
                ins.then_inc(bn_done, 1)

            def norm(t, u):
                m = LN_IDX[u]
                s = m % 3
                n = NLN * t + m
                ve.wait_ge(coef_done, n + 1)
                if m >= 3 or not (isinstance(t, int) and t == 0):
                    ve.wait_ge(headT_done, n - 2)
                for h in range(4):
                    ins = ve.tensor_scalar(nrm[s][:, h * D:(h + 1) * D], raw[s][:, h * D:(h + 1) * D],
                                           cw[:, s, h:h + 1], cb[:, s, h:h + 1], ALU.mult,
                                           ALU.subtract)
                ins.then_inc(norm_done, 1)

            def softmax_in(w, c):
                s3 = score_ps[:, :].rearrange("p (g t) -> p g t", t=S)
                ve.wait_ge(score_done, w + 1)
                ve.tensor_reduce(mx[:, :], s3, AX.X, ALU.max).then_inc(max_done, 1)
                ve.wait_ge(max_done, w + 1)
                ge(ve, probn_done, w - 1)
                ve.tensor_tensor(prob[c % 2].rearrange("p (g t) -> p g t", t=S), s3,
                                 mx[:, :].unsqueeze(2).to_broadcast([P, 8, S]),
                                 ALU.subtract).then_inc(sub_done, 1)

            def softmax_sum(w, c):
                ve.wait_ge(exp_done, w + 1)
                ve.tensor_reduce(sm[:, :], prob[c % 2].rearrange("p (g t) -> p g t", t=S), AX.X,
                                 ALU.add).then_inc(sum_done, 1)
                ve.wait_ge(sum_done, w + 1)
                ve.reciprocal(rinv[:, c % 2, :], sm[:, :]).then_inc(rinv_done, 1)

            def quantise(w, c):
                ve.wait_ge(pv_done, w + 1)
                y3 = yv[:, :].rearrange("p (h t) -> p h t", t=P)
                for b in range(2):
                    ins = ve.tensor_tensor(y3[:, :, b * S:(b + 1) * S],
                                           pv_ps[b][:, :].rearrange("p (h t) -> p h t", t=S),
                                           smi[:, 8 * c:8 * c + 8].unsqueeze(2).to_broadcast([P, 8, S]),
                                           ALU.mult)
                ins.then_inc(y_done, 1)
                ve.wait_ge(y_done, w + 1)
                ve.tensor_scalar(yv[:, :], yv[:, :], FP8_MAX, -FP8_MAX, ALU.min, ALU.max)\
                  .then_inc(clip_done, 1)
                to_grid(catq[c % 2], lambda: ge(ve, op_done, w - 1), catq_done, Q0 + w + 1)

            def residual(t):
                ve.wait_ge(op_done, NU * (t + 1))
                xt = xs[:, bass.ds(t * H, H)]
                ve.scalar_tensor_tensor(xt, out_ps[:, 0:H], gate[:, 2:3], xt, ALU.mult, ALU.add)\
                  .then_inc(res_done, 1)

            def step(tb, tc, c, prev=None):
                if tc is not None:
                    softmax_in(NU * tc + c, c)
                if tb is not None:
                    stats(tb, 4 * c)
                    stats(tb, 4 * c + 1)
                if tc is not None:
                    softmax_sum(NU * tc + c, c)
                if tb is not None:
                    norm(tb, 4 * c)
                    stats(tb, 4 * c + 2)
                    norm(tb, 4 * c + 1)
                if c > 0 and tc is not None:
                    quantise(NU * tc + c - 1, c - 1)
                elif prev is not None:
                    quantise(NU * prev + NU - 1, NU - 1)
                if tb is not None:
                    norm(tb, 4 * c + 2)
                if prev is not None:
                    residual(prev)

            for c in range(NU):
                step(0, None, c)
            for c in range(NU):
                step(1, 0, c)
            with ve.Fori(0, (NT - 2) // 2) as i:
                for d in range(2):
                    for c in range(NU):
                        tc = 2 * i + 1 + d
                        step(tc + 1, tc, c, prev=(tc - 1) if c == 0 else None)
            for c in range(NU):
                step(None, NT - 1, c, prev=NT - 2 if c == 0 else None)
            quantise(NU * NT - 1, NU - 1)
            residual(NT - 1)

            ve.wait_ge(res_done, NT)
            row_stats()
            link(ve.tensor_scalar(tw[:, 0, :], var, EPS, None, ALU.add))
            ve.tensor_scalar(tw[:, 3, :], var, 1.0, None, ALU.mult).then_inc(ln_in, 1)
            ve.wait_ge(ln_root, 3)
            newton(tw[:, 2, :], tw[:, 0, :], tw[:, 4, :], tw[:, 5, :])
            link(ve.tensor_copy(tn[:, 0, :], tw[:, 2, :]))
            link(ve.scalar_tensor_tensor(tn[:, 1, :], mean, -1.0, tn[:, 0, :], ALU.mult, ALU.mult))
            row_norm()
            for k in range(4):
                c, half = k // 2, k % 2
                sl = slice(half * 512, half * 512 + 512)
                ve.wait_ge(xT_evac, 4 + k + 1)
                ve.tensor_tensor(zl[:, c, sl], zT[:, c, sl], zh[:, c, sl], ALU.subtract).then_inc(zl_done, 1)
            link(ve.tensor_copy(idb, idf[:, :]))
            ve.wait_ge(logit_done, 1)
            L3 = proj_ps[0][:, 0:NT * NE].rearrange("p (t e) -> p t e", t=NT)
            logits, biased, ex, m1, m2, comb, rem, rem2, _sp = rt
            link(ve.tensor_copy(logits, L3))
            ve.tensor_tensor(biased, logits, rowv[:, 0:NE].unsqueeze(1).to_broadcast([P, NT, NE]), ALU.add)
            link(ve.tensor_reduce(rs8[:, 0, :], logits, AX.X, ALU.max))
            ve.tensor_tensor(ex, logits, rs8[:, 0, :].unsqueeze(2).to_broadcast([P, NT, NE]),
                             ALU.subtract).then_inc(rexp_in, 1)
            for t in range(NT):
                ins = ve.max(m8[:, t, :], biased[:, t, :])
            link(ins)
            for t in range(NT):
                ins = ve.max_index(i8[:, t, :], m8[:, t, :], biased[:, t, :])
            link(ins)
            link(ve.tensor_copy(i8f, i8))
            iota = rowv[:, NE:2 * NE].unsqueeze(1).to_broadcast([P, NT, NE])
            ve.tensor_tensor(m1, iota, i8f[:, :, 0:1].to_broadcast([P, NT, NE]), ALU.is_equal)
            link(ve.tensor_tensor(m2, iota, i8f[:, :, 1:2].to_broadcast([P, NT, NE]), ALU.is_equal))
            link(ve.tensor_tensor(m1, m1, m2, ALU.add))
            ve.wait_ge(rexp_done, 1)
            link(ve.tensor_tensor(m2, ex, m1, ALU.mult))
            link(ve.tensor_reduce(rs8[:, 1, :], m2, AX.X, ALU.add))
            link(ve.reciprocal(rs8[:, 2, :], rs8[:, 1, :]))
            link(ve.tensor_tensor(comb, m2, rs8[:, 2, :].unsqueeze(2).to_broadcast([P, NT, NE]), ALU.mult))
            link(ve.tensor_copy(cbt[:, :, 0:NE], comb))
            link(ve.tensor_tensor(rem, comb, cbt[:, :, 0:NE], ALU.subtract))
            link(ve.tensor_copy(cbt[:, :, NE:2 * NE], rem))
            link(ve.tensor_tensor(rem2, rem, cbt[:, :, NE:2 * NE], ALU.subtract))
            link(ve.tensor_copy(cbt[:, :, 2 * NE:3 * NE], rem2))
            ve.memset(cbt[:, :, 3 * NE:4 * NE], 1.0).then_inc(comb_done, 1)
            ve.wait_ge(combT_done, 1)
            ve.tensor_copy(combT, headT_ps[:, :].bitcast(BF16)[0:NROW, :]).then_inc(combT_evac, 1)

            def split_lo(n, par):
                ve.wait_ge(we_hi, n + 1)
                ve.scalar_tensor_tensor(wel[par], wst[par], WF_SCALE, weh[par], ALU.mult,
                                        ALU.subtract).then_inc(we_lo, 1)

            def hidden(n, par):
                ve.wait_ge(silu_done, n + 1)
                ve.scalar_tensor_tensor(ht[par], ups[par][1][:, :], 1.0 / WF_SCALE, hs[par], ALU.mult,
                                        ALU.mult).then_inc(prod_done, 1)
                ve.wait_ge(prod_done, n + 1)
                ge(ve, hid_lo, n - 1)
                ge(ve, hid_hi, n - 1)
                ve.tensor_tensor(hf[par], ht[par], ups[par][2][:, :], ALU.mult).then_inc(hid_done, 1)

            def results(half):
                ve.wait_ge(down_done, NX * (half + 1))
                for j in range(4):
                    t = 4 * half + j
                    ve.scalar_tensor_tensor(yo[t], pv_ps[j // 2][:, (j % 2) * H:(j % 2) * H + H],
                                            gate[:, 1:2], xs[:, t * H:(t + 1) * H], ALU.mult,
                                            ALU.add).then_inc(y_ready, 1)

            split_lo(0, 0)
            def pair(n, last=False):
                split_lo(n + 1, 1)
                hidden(n, 0)
                if not last:
                    split_lo(n + 2, 0)
                hidden(n + 1, 1)
            pair(0)
            with ve.Fori(1, NX // 2) as i:
                pair(2 * i)
            results(0)
            with ve.Fori(0, NX // 2 - 1) as i:
                pair(NX + 2 * i)
            pair(2 * NX - 2, last=True)
            results(1)


def kernel(**inputs):
    import concourse.bacc as bacc
    from concourse.bass_utils import run_bass_kernel_spmd as run

    v = {k: np.asarray(a) for k, a in inputs.items()}
    at = {k[len("L0_xattn_"):]: a for k, a in v.items() if k.startswith("L0_xattn_")}
    ff = {k[len("L0_ffn_"):]: a for k, a in v.items() if k.startswith("L0_ffn_")}

    def per_row(a):
        return np.ascontiguousarray(a.reshape(-1, P).T)

    def everywhere(a):
        return np.broadcast_to(a.reshape(1, 1), (P, 1))

    cols = np.concatenate(
        [per_row(at[k]) for k in ("ln_w", "ln_b", "k_in_scale", "q_in_scale", "v_in_scale", "qx_in_scale",
                                  "qln_w", "kln_w", "qxln_w", "kxln_w", "qln_b", "kln_b", "qxln_b", "kxln_b",
                                  "proj_smooth")]
        + [everywhere(a) for a in (at["wq_scale"], at["wk_scale"], at["wqx_scale"], at["wv_scale"],
                                   at["proj_w_scale"], at["proj_in_scale"], v["g_xattn"], v["g_ffn"])], axis=1)
    rowc = np.concatenate([np.broadcast_to(ff["router_bias"][None, :], (P, NE)),
                           np.broadcast_to(np.arange(NE, dtype=np.float32)[None, :], (P, NE))], axis=1)
    sel = np.zeros((NROW, NX, P), np.float32)
    for e in range(NX):
        for r in ((e, NE + e, 2 * NE + e) if e < NE else (3 * NE,)):
            sel[r, e, :] = 1.0

    def up(we, ws):
        a = np.concatenate([we.transpose(1, 0, 2).reshape(H, NE * FE), ws[0]], axis=1)
        return a.reshape(HC, P, NX, FE).transpose(2, 1, 0, 3).reshape(NX, P, HC * FE)

    wffn = np.concatenate([up(ff["Wu"], ff["Su"]), up(ff["Wg"], ff["Sg"]),
                           np.concatenate([ff["Wd"], ff["Sd"][0].reshape(NSH, FE, H)], axis=0)], axis=2)
    arrays = {
        "x": v["x"].reshape(TOK, H), "cols": cols, "rowc": rowc, "ident": np.eye(P, dtype=np.float32),
        "sel": sel.reshape(NROW, NX * P), "ctxT": v["ctx_2048"].reshape(TOK, H).T,
        "wkvT": at["w_kv_x"].T, "wqT": at["wq"].T, "wkT": at["wk"].T, "wvT": at["wv"].T,
        "wqxT": at["wqx"].T, "wpT": at["wproj"].T, "rwT": ff["router_w"].T, "wffn": wffn,
    }
    nc = bacc.Bacc("TRN2", target_bir_lowering=False, num_devices=1)
    feed, args = {}, []
    for name, a in arrays.items():
        a = np.ascontiguousarray(a)
        feed["in_" + name] = a
        args.append(nc.dram_tensor("in_" + name, a.shape, mybir.dt.from_np(a.dtype), kind="ExternalInput").ap())
    args.append(nc.dram_tensor("out_y", (TOK, H), F32, kind="ExternalOutput").ap())
    build(nc, *args)
    r = run(nc, [feed], core_ids=[0])
    return r.results[0]["out_y"].reshape(NB, S, H)
```

```python
from contextlib import ExitStack

import numpy as np

import concourse.bass as bass
from concourse import mybir

F32 = mybir.dt.float32
F16 = mybir.dt.float16
BF16 = mybir.dt.bfloat16
U16 = mybir.dt.uint16
U32 = mybir.dt.uint32
ALU = mybir.AluOpType
ACT = mybir.ActivationFunctionType
AX = mybir.AxisListType

P = 128
NB, S, H = 16, 64, 256
TOK = NB * S
NT = TOK // P
HC = H // P
D = 128
NH, G = 16, 8
NE, TOPK, FE = 16, 2, 128
NSH = 2
NX = NE + NSH
EPS = 1e-5
FP8_MAX = 448.0
SCORE_SCALE = 1.0 / float(np.sqrt(D))
WKV_SCALE = 64.0
WF_SCALE = 16.0
NROW = 3 * NE + 1

COL = {}
_n = 0
for _name, _w in (("lnw", HC), ("lnb", HC), ("in_k", HC), ("in_q", HC), ("in_v", HC), ("in_qx", HC),
                  ("qw", 1), ("kw", 1), ("qxw", 1), ("kxw", 1), ("qb", 1), ("kb", 1), ("qxb", 1), ("kxb", 1),
                  ("smooth", 2 * NH), ("s_q", 1), ("s_k", 1), ("s_qx", 1), ("s_v", 1),
                  ("s_proj", 1), ("s_pin", 1), ("g_x", 1), ("g_f", 1)):
    COL[_name] = (_n, _n + _w)
    _n += _w
NCOL = _n

BANKS = [("k", 0), ("q", 0), ("q", 1), ("v", 0),
         ("k", 1), ("q", 2), ("q", 3), ("v", 1),
         ("kx", 0), ("qx", 0), ("qx", 1), ("vx", 0),
         ("kx", 1), ("qx", 2), ("qx", 3), ("vx", 1)]
XORDER = ("k", "q", "v", "qx")


def ge(eng, sem, value):
    if isinstance(value, int) and value <= 0:
        return
    eng.wait_ge(sem, value)


def live(n, back):
    return not isinstance(n, int) or 0 <= n - back < 4 * NT


def run_steps(eng, step):
    for c in range(4):
        step(0, c)
    with eng.Fori(1, NT - 1) as t:
        for c in range(4):
            step(t, c)
    for n in range(4 * (NT - 1), 4 * NT + 4):
        step(n // 4, n % 4)


def build(nc, x, cols, rowc, ident, sel, ctxT, wkvT, wqT, wkT, wvT, wqxT, wpT, rwT, wffn, out):
    ctx = ExitStack()
    with ctx:
        def sb(name, shape, dt):
            return ctx.enter_context(nc.sbuf_tensor(name, shape, dt))

        def bank(name):
            return ctx.enter_context(nc.psum_tensor(name, [P, 512], F32))

        def sem(name):
            return ctx.enter_context(nc.semaphore(name))

        NU = 4
        XW = 4 * HC * P

        proj_ps = [bank("proj_ps0"), bank("proj_ps1")]
        headT_ps = bank("headT_ps")
        probT_ps = bank("probT_ps")
        score_ps = bank("score_ps")
        pv_ps = [bank("pv_ps0"), bank("pv_ps1")]
        out_ps = bank("out_ps")
        wide_ps = [score_ps, out_ps, pv_ps[0], pv_ps[1]]

        xs = sb("xs", [P, NT * H], F32)
        colv = sb("colv", [P, NCOL], F32)
        rowv = sb("rowv", [P, 2 * NE], F32)
        idf = sb("idf", [P, P], F32)
        XHf = sb("XH", [P, NT * XW], F16)
        XLf = sb("XL", [P, NT * XW], F16)
        ctxh = sb("ctxh", [P, HC, TOK], F16)
        ctxl = sb("ctxl", [P, HC, TOK], F16)
        wkvh = sb("wkvh", [P, HC, 2 * G * D], F16)
        wkvl = sb("wkvl", [P, HC, 2 * G * D], F16)
        wb = {"q": sb("wq_sb", [P, HC, NH * D], BF16), "k": sb("wk_sb", [P, HC, G * D], BF16),
              "v": sb("wv_sb", [P, HC, G * D], BF16), "qx": sb("wqx_sb", [P, HC, NH * D], BF16)}
        wp = sb("wp_sb", [P, 2 * NH, H], BF16)
        rot = sb("rot", [P, 6, 512], F32)
        raw = [[rot[:, 3 * i + b, :] for b in range(3)] for i in range(2)]
        xn = rot[:, 0:4, :].rearrange("p a b -> p (a b)")
        xT = sb("xT", [P, HC, TOK], F32)
        xin = sb("xin", [P, XW], BF16)
        xpr = sb("xpr", [P, XW], F32)
        qT = sb("qT", [P, 2, 8, P], F32)
        kT = sb("kT", [P, 2, 4, P], F32)
        vf = sb("vf", [P, 2, 512], F32)
        vh = sb("vh", [P, NU, 512], F16)
        vl16 = sb("vl16", [P, NU, 512], F16)
        wkv_stage = sb("wkv_stage", [P, 4096], F32)
        reg1 = sb("reg1", [P, 2048], F32)
        reg2 = sb("reg2", [P, 2048], F32)
        prob = [reg1[:, 512 * i:512 * i + 512] for i in range(2)]
        probn = [reg1[:, 1024 + 512 * i:1536 + 512 * i] for i in range(2)]
        ctx_st = reg2[:, :]
        probT = [reg2[:, 512 * i:512 * i + 512].bitcast(F16) for i in range(2)]
        catq = [reg2[:, 1024 + 512 * i:1536 + 512 * i].bitcast(BF16) for i in range(2)]
        wkv_st = wkv_stage[:, :]
        probs = sb("probs", [P, 2, 1024], F16)
        idh = sb("idh", [P, P], F16)
        yv = sb("yv", [P, 1024], BF16)
        ya = sb("ya", [P, 1024], BF16)
        ym = sb("ym", [P, 1024], F16)
        ys = sb("ys", [P, 1024], F16)
        mx = sb("mx", [P, 8], F32)
        sm = sb("sm", [P, 8], F32)
        rinv = sb("rinv", [P, 2, 8], F32)
        NLH = 12
        st = sb("st", [P, NLH, 6], F32)
        mean2 = sb("mean2", [P, NLH], F32)
        vw = sb("vw", [P, 6, NLH], F32)
        va = sb("va", [P, NLH], F32)
        vl = sb("vl", [P, NLH], F32)
        r0 = sb("r0", [P, NLH], F32)
        nw = sb("nw", [P, 5, NLH], F32)
        cw = sb("cw", [P, NLH], F32)
        cb = sb("cb", [P, NLH], F32)
        sinv = sb("sinv", [P, 4 * HC], F32)
        smi = sb("smi", [P, 2 * NH], F32)
        lnC = sb("lnC", [P, 6, 2, NLH], F32)
        lnW = sb("lnW", [P, 2, NLH], F32)
        th = sb("th", [P, 2], F32)
        gate = sb("gate", [P, 3], F32)
        tst = sb("tst", [P, NT, 6], F32)
        tmv = sb("tmv", [P, NT, 2], F32)
        tw = sb("tw", [P, 8, NT], F32)
        tn = sb("tn", [P, 2, NT], F32)

        NS = 4
        zh = XHf[:, 0:2048].rearrange("p (c t) -> p c t", c=HC)
        zl = XHf[:, 2048:4096].rearrange("p (c t) -> p c t", c=HC)
        zT = XLf[:, 0:4096].bitcast(F32).rearrange("p (c t) -> p c t", c=HC)
        WE = 3 * H
        wst = [XLf[:, 4096 + 2 * WE * i:4096 + 2 * WE * (i + 1)].bitcast(F32) for i in range(2)]
        weh, wel = [[a[:, :, :].rearrange("p c o -> p (c o)")[:, WE * i:WE * (i + 1)] for i in range(NS)]
                    for a in (wkvh, wkvl)]
        hs = [wkv_stage[:, 512 * i:512 + 512 * i] for i in range(2)]
        ht = [wkv_stage[:, 1024 + 512 * i:1536 + 512 * i] for i in range(2)]
        hf = [XHf[:, 4096 + 1024 * i:5120 + 1024 * i].bitcast(F32) for i in range(2)]
        hh = [XHf[:, 6144 + 512 * i:6656 + 512 * i] for i in range(NS)]
        hl = [reg1[:, 256 * i:256 * i + 256].bitcast(F16) for i in range(NS)]
        yo = [wkv_stage[:, 2048 + 256 * i:2304 + 256 * i] for i in range(NT)]
        tail = wb["qx"][:, :, :].rearrange("p c o -> p (c o)").bitcast(F32)
        sel_sb = tail[0:NROW, 0:NX * P // 2].bitcast(BF16).rearrange("p (e m) -> p e m", e=NX)
        combT = tail[0:NROW, 1152:1664].bitcast(BF16)
        idb = tail[:, 1664:1728].bitcast(BF16)
        rws = tail[:, 1728:1760].rearrange("p (c e) -> p c e", c=HC)
        NTE = NT * NE
        vff = vf[:, :, :].rearrange("p a b -> p (a b)")
        vhf = vh[:, :, :].rearrange("p a b -> p (a b)").bitcast(F32)
        rt = [vff[:, NTE * i:NTE * (i + 1)].rearrange("p (t e) -> p t e", t=NT) for i in range(8)]
        m8 = vhf[:, 0:64].rearrange("p (t k) -> p t k", t=NT)
        i8 = vhf[:, 64:128].bitcast(U32).rearrange("p (t k) -> p t k", t=NT)
        i8f = vhf[:, 128:192].rearrange("p (t k) -> p t k", t=NT)
        rs8 = vhf[:, 192:216].rearrange("p (a t) -> p a t", a=3)
        cbt = vhf[:, 256:256 + NT * 32].bitcast(BF16).rearrange("p (t e) -> p t e", t=NT)

        def col(name, c=0):
            a = COL[name][0] + c
            return colv[:, a:a + 1]

        ld_x = sem("ld_x")
        ld_small = sem("ld_small")
        ld_ctx = sem("ld_ctx")
        ld_wkv = sem("ld_wkv")
        ld_w = {k: sem("ld_w" + k) for k in ("k", "q", "v", "qx")}
        ld_wp = sem("ld_wp")
        ld_tail = sem("ld_tail")
        prep_done = sem("prep_done")
        tanh_done = sem("tanh_done")
        ln_in = sem("ln_in")
        ln_mid = sem("ln_mid")
        ln_root = sem("ln_root")
        dchain = sem("dchain")
        xn_done = sem("xn_done")
        xT_done = sem("xT_done")
        xT_evac = sem("xT_evac")
        xin_done = sem("xin_done")
        xclip_done = sem("xclip_done")
        xabs_done = sem("xabs_done")
        xmag_done = sem("xmag_done")
        xbig_done = sem("xbig_done")
        xgrid_done = sem("xgrid_done")
        xpr_done = sem("xpr_done")
        xhi_done = sem("xhi_done")
        xs_ready = sem("xs_ready")
        ctx_hi = sem("ctx_hi")
        ctx_ready = sem("ctx_ready")
        wkv_hi = sem("wkv_hi")
        wkv_ready = sem("wkv_ready")
        proj_done = sem("proj_done")
        proj_evac = sem("proj_evac")
        bn_done = sem("bn_done")
        achain = sem("achain")
        var_done = sem("var_done")
        log_done = sem("log_done")
        root_done = sem("root_done")
        nchain = sem("nchain")
        coef_done = sem("coef_done")
        norm_done = sem("norm_done")
        norm2_done = sem("norm2_done")
        headT_done = sem("headT_done")
        headT_evac = sem("headT_evac")
        score_done = sem("score_done")
        max_done = sem("max_done")
        sub_done = sem("sub_done")
        exp_done = sem("exp_done")
        sum_done = sem("sum_done")
        rinv_done = sem("rinv_done")
        probn_done = sem("probn_done")
        prob_hi = sem("prob_hi")
        prob_lo = sem("prob_lo")
        v_hi = sem("v_hi")
        v_lo = sem("v_lo")
        idh_done = sem("idh_done")
        probT_done = sem("probT_done")
        probT_evac = sem("probT_evac")
        pv_done = sem("pv_done")
        y_done = sem("y_done")
        clip_done = sem("clip_done")
        abs_done = sem("abs_done")
        mag_done = sem("mag_done")
        big_done = sem("big_done")
        catq_done = sem("catq_done")
        op_done = sem("op_done")
        res_done = sem("res_done")
        zl_done = sem("zl_done")
        logit_done = sem("logit_done")
        rexp_in = sem("rexp_in")
        rexp_done = sem("rexp_done")
        comb_done = sem("comb_done")
        combT_done = sem("combT_done")
        combT_evac = sem("combT_evac")
        idb_done = sem("idb_done")
        we_ld = [sem("we_ld0"), sem("we_ld1")]
        we_hi = sem("we_hi")
        we_lo = sem("we_lo")
        up_done = sem("up_done")
        silu_done = sem("silu_done")
        prod_done = sem("prod_done")
        hid_done = sem("hid_done")
        hid_hi = sem("hid_hi")
        hid_lo = sem("hid_lo")
        down_done = sem("down_done")
        y_ready = sem("y_ready")
        stored = sem("stored")

        ups = [(proj_ps[0], headT_ps, score_ps), (proj_ps[1], probT_ps, out_ps)]
        block = ctx.enter_context(nc.Block())
        @block.sync
        def _(sp):
            sp.dma_start(xs[:, :].rearrange("p (t d) -> p t d", t=NT),
                         x.rearrange("(t p) d -> p t d", p=P)).then_inc(ld_x, 16)
            sp.dma_start(colv[:, :], cols).then_inc(ld_small, 16)
            sp.dma_start(rowv[:, :], rowc).then_inc(ld_small, 16)
            sp.dma_start(idf[:, :], ident).then_inc(ld_small, 16)
            sp.dma_start(ctx_st.rearrange("p (c t) -> p c t", c=HC),
                         ctxT.rearrange("(c p) t -> p c t", p=P)).then_inc(ld_ctx, 16)
            sp.dma_start(wkv_st.rearrange("p (c t) -> p c t", c=HC),
                         wkvT.rearrange("(c p) t -> p c t", p=P)).then_inc(ld_wkv, 16)
            sp.wait_ge(proj_done, 4 * NU * NT)

            def load(e, n, par):
                ge(sp, we_lo, n - 1)
                ge(sp, we_hi, n - 1)
                sp.dma_start(wst[par], wffn[bass.ds(e, 1), :, :].rearrange("a p n -> p (a n)")
                             if not isinstance(e, int) else wffn[e, :, :]).then_inc(we_ld[par], 16)

            load(0, 0, 0)
            load(1, 1, 1)
            with sp.Fori(1, NX // 2) as i:
                load(2 * i, 2 * i, 0)
                load(2 * i + 1, 2 * i + 1, 1)
            with sp.Fori(0, NX // 2) as i:
                load(2 * i, NX + 2 * i, 0)
                load(2 * i + 1, NX + 2 * i + 1, 1)
            for t in range(NT):
                sp.wait_ge(y_ready, t + 1)
                sp.dma_start(out[t * P:(t + 1) * P, :], yo[t]).then_inc(stored, 16)
            sp.wait_ge(stored, 16 * NT)

        @block.gpsimd
        def _(gp):
            for k, w in (("k", wkT), ("q", wqT), ("v", wvT), ("qx", wqxT)):
                gp.dma_start(wb[k][:, :, :], w.rearrange("(c p) o -> p c o", p=P)).then_inc(ld_w[k], 16)
            gp.dma_start(wp[:, :, :], wpT.rearrange("(h p) o -> p h o", p=P)).then_inc(ld_wp, 16)

            def tile_of(buf, T):
                return buf[:, bass.ds(T * XW, XW)]

            def inputs_over_scale(T):
                gp.wait_ge(xT_evac, 4)
                ge(gp, xpr_done, T)
                gp.tensor_tensor(xin[:, :].rearrange("p (j c t) -> p j c t", j=4, c=HC),
                                 xT[:, :, bass.ds(T * P, P)].unsqueeze(1).to_broadcast([P, 4, HC, P]),
                                 sinv[:, :].rearrange("p (j c) -> p j c", j=4).unsqueeze(3)
                                 .to_broadcast([P, 4, HC, P]), ALU.mult).then_inc(xin_done, 1)

            def inputs_times_scale(T):
                gp.wait_ge(xgrid_done, T + 1)
                ge(gp, xs_ready, T)
                a0 = COL["in_k"][0]
                gp.tensor_tensor(xpr[:, :].rearrange("p (n t) -> p n t", t=P),
                                 xin[:, :].rearrange("p (n t) -> p n t", t=P),
                                 colv[:, a0:a0 + 4 * HC].unsqueeze(2).to_broadcast([P, 4 * HC, P]),
                                 ALU.mult).then_inc(xpr_done, 1)

            def inputs_low(T):
                gp.wait_ge(xhi_done, T + 1)
                gp.tensor_tensor(tile_of(XLf, T), xpr[:, :], tile_of(XHf, T),
                                 ALU.subtract).then_inc(xs_ready, 1)

            gp.wait_ge(prep_done, 1)
            inputs_over_scale(0)
            inputs_times_scale(0)
            inputs_low(0)
            gp.wait_ge(ctx_hi, 1)
            gp.tensor_tensor(ctxl[:, :, :].rearrange("p c t -> p (c t)"), ctx_st,
                             ctxh[:, :, :].rearrange("p c t -> p (c t)"), ALU.subtract).then_inc(ctx_ready, 1)
            def chained(sem, ins, count):
                ins.then_inc(sem, 1)
                gp.wait_ge(sem, count)

            def variance(n, x):
                gp.wait_ge(bn_done, n + 1)
                ge(gp, coef_done, n)
                even, odd = st[:, :, 1], st[:, :, 4]
                gp.tensor_tensor(mean2[:, :], even, odd, ALU.add)
                gp.tensor_tensor(vw[:, 0, :], st[:, :, 2], st[:, :, 5], ALU.add)
                chained(achain, gp.tensor_tensor(vw[:, 1, :], even, odd, ALU.subtract), 4 * n + 1)
                gp.tensor_tensor(vw[:, 3, :], vw[:, 0, :], lnC[:, 0, x, :], ALU.mult)
                chained(achain, gp.tensor_tensor(vw[:, 2, :], vw[:, 1, :], vw[:, 1, :], ALU.mult), 4 * n + 2)
                chained(achain, gp.tensor_tensor(vw[:, 4, :], vw[:, 2, :], lnC[:, 1, x, :], ALU.mult),
                        4 * n + 3)
                chained(achain, gp.tensor_tensor(vw[:, 5, :], vw[:, 3, :], vw[:, 4, :], ALU.add), 4 * n + 4)
                gp.tensor_tensor(va[:, :], vw[:, 5, :], lnC[:, 2, x, :], ALU.add).then_inc(var_done, 1)

            def coefficients(n, x):
                gp.wait_ge(root_done, n + 1)
                chained(nchain, gp.tensor_tensor(nw[:, 0, :], va[:, :], r0[:, :], ALU.mult), 5 * n + 1)
                chained(nchain, gp.tensor_tensor(nw[:, 1, :], nw[:, 0, :], r0[:, :], ALU.mult), 5 * n + 2)
                chained(nchain, gp.tensor_tensor(nw[:, 2, :], nw[:, 1, :], lnC[:, 3, x, :], ALU.mult),
                        5 * n + 3)
                gp.tensor_tensor(nw[:, 4, :], mean2[:, :], lnC[:, 5, x, :], ALU.mult)
                chained(nchain, gp.tensor_tensor(nw[:, 3, :], nw[:, 2, :], lnC[:, 4, x, :], ALU.add),
                        5 * n + 4)
                ge(gp, norm_done, 2 * n)
                ge(gp, norm2_done, n)
                chained(nchain, gp.tensor_tensor(cw[:, :], nw[:, 3, :], r0[:, :], ALU.mult), 5 * n + 5)
                gp.tensor_tensor(cb[:, :], nw[:, 4, :], cw[:, :], ALU.mult).then_inc(coef_done, 1)

            def normalise(w, s):
                gp.wait_ge(rinv_done, w + 1)
                ge(gp, prob_lo, w - 1)
                gp.tensor_tensor(probn[s].rearrange("p (g t) -> p g t", t=S),
                                 prob[s].rearrange("p (g t) -> p g t", t=S),
                                 rinv[:, s, :].unsqueeze(2).to_broadcast([P, 8, S]),
                                 ALU.mult).then_inc(probn_done, 1)

            def prob_low(w, s):
                gp.wait_ge(prob_hi, w + 1)
                gp.tensor_tensor(probs[:, s, 512:1024], probn[s], probs[:, s, 0:512],
                                 ALU.subtract).then_inc(prob_lo, 1)

            def value_low(n, c):
                gp.wait_ge(v_hi, n + 1)
                gp.tensor_tensor(vl16[:, c, :], vf[:, c % 2, :], vh[:, c, :], ALU.subtract).then_inc(v_lo, 1)

            def step(t, c):
                n = NU * t + c
                if live(n, 2):
                    normalise(n - 2, c % 2)
                    prob_low(n - 2, c % 2)
                if live(n, 0):
                    if c == 0 and live(n, -NU):
                        inputs_over_scale(t + 1)
                    if c == 2 and live(n, -NU):
                        inputs_times_scale(t + 1)
                    variance(n, c // 2)
                    coefficients(n, c // 2)
                    if c == 3 and live(n, -1):
                        inputs_low(t + 1)
                    value_low(n, c)

            run_steps(gp, step)
            gp.wait_ge(proj_done, 4 * NU * NT)
            gp.dma_start(tail[0:NROW, 0:NX * P // 2].bitcast(BF16), sel).then_inc(ld_tail, 16)
            gp.dma_start(rws, rwT.rearrange("(c p) e -> p c e", p=P)).then_inc(ld_tail, 16)
            def low(n, j):
                gp.wait_ge(hid_hi, n + 1)
                ge(gp, down_done, n - 3)
                gp.tensor_tensor(hl[j % 4], hf[j % 2], hh[j % 4], ALU.subtract).then_inc(hid_lo, 1)

            for n in range(4):
                low(n, n)
            with gp.Fori(1, NX // 2) as i:
                for j in range(4):
                    low(4 * i + j, j)

        @block.scalar
        def _(act):
            act.wait_ge(ld_small, 48)
            a = COL["g_x"][0]
            act.activation(th[:, :], colv[:, a:a + 2], ACT.Tanh).then_inc(tanh_done, 1)

            act.preload_act_table_set("natural_log_exp_and_others")

            def root(n, src, mid, dst):
                act.wait_ge(ln_in, n + 1)
                act.activation(mid, src, ACT.Ln).then_inc(ln_mid, 1)
                act.wait_ge(ln_mid, n + 1)
                act.activation(dst, mid, ACT.Exp, scale=-0.5).then_inc(ln_root, 1)

            act.wait_ge(ld_ctx, 16)
            act.activation(ctxh[:, :, :].rearrange("p c t -> p (c t)"), ctx_st, ACT.Copy).then_inc(ctx_hi, 1)
            root(0, tw[:, 0, :], tw[:, 1, :], tw[:, 2, :])
            root(1, tw[:, 0, :], tw[:, 1, :], tw[:, 2, :])
            for k in range(4):
                c, half = k // 2, k % 2
                act.wait_ge(xT_done, k + 1)
                act.activation(xT[:, c, half * 512:half * 512 + 512], wide_ps[k][:, :], ACT.Identity,
                               scale=col("lnw", c), bias=col("lnb", c)).then_inc(xT_evac, 1)
            def inputs_high(T):
                act.wait_ge(xpr_done, T + 1)
                act.activation(XHf[:, bass.ds(T * XW, XW)], xpr[:, :], ACT.Copy).then_inc(xhi_done, 1)

            inputs_high(0)
            act.wait_ge(ld_wkv, 16)
            act.activation(wkvh[:, :, :].rearrange("p c t -> p (c t)"), wkv_st, ACT.Copy,
                           scale=WKV_SCALE).then_inc(wkv_hi, 1)

            def evacuate(n, c, i):
                act.wait_ge(proj_done, 4 * n + i + 1)
                ge(act, headT_done, 3 * (n - 2) + i + 1)
                act.activation(raw[c % 2][i], proj_ps[i % 2][:, :], ACT.Copy).then_inc(proj_evac, 1)

            def evacuate_values(t, c):
                n = NU * t + c
                act.wait_ge(proj_done, 4 * n + 4)
                ge(act, v_lo, n - 1)
                scale = col("s_v") if c < 2 else 1.0 / WKV_SCALE
                act.activation(vf[:, c % 2, :], proj_ps[1][:, :], ACT.Copy, scale=scale).then_inc(proj_evac, 1)
                act.wait_ge(proj_evac, 4 * n + 4)
                ge(act, pv_done, n - 3)
                act.activation(vh[:, c, :], vf[:, c % 2, :], ACT.Copy).then_inc(v_hi, 1)

            def roots(n):
                act.wait_ge(var_done, n + 1)
                act.activation(vl[:, :], va[:, :], ACT.Ln).then_inc(log_done, 1)
                act.wait_ge(log_done, n + 1)
                act.activation(r0[:, :], vl[:, :], ACT.Exp, scale=-0.5).then_inc(root_done, 1)

            def norm_bank2(n, c):
                act.wait_ge(coef_done, n + 1)
                for h in range(4):
                    r = raw[c % 2][2][:, h * D:(h + 1) * D]
                    ins = act.activation(r, r, ACT.Identity, scale=cw[:, 8 + h:9 + h], bias=cb[:, 8 + h:9 + h])
                ins.then_inc(norm2_done, 1)

            def heads_out(n, c, i):
                kind, b = BANKS[4 * c + i]
                act.wait_ge(headT_done, 3 * n + i + 1)
                ge(act, score_done, n - 1)
                if kind in ("q", "qx"):
                    dst = qT[:, c % 2, 4 * (b % 2):4 * (b % 2) + 4, :]
                else:
                    dst = kT[:, c % 2, :, :]
                act.activation(dst, headT_ps[:, :].rearrange("p (h t) -> p h t", h=4), ACT.Identity,
                               scale=col(kind + "w"), bias=col(kind + "b")).then_inc(headT_evac, 1)

            def expo(w, s):
                act.wait_ge(sub_done, w + 1)
                act.activation(prob[s], prob[s], ACT.Exp, scale=SCORE_SCALE).then_inc(exp_done, 1)

            def prob_high(w, s):
                act.wait_ge(probn_done, w + 1)
                ge(act, probT_done, w - 1)
                act.activation(probs[:, s, 0:512], probn[s], ACT.Copy).then_inc(prob_hi, 1)

            def prob_out(w, s):
                act.wait_ge(probT_done, w + 1)
                ge(act, pv_done, w - 1)
                act.activation(probT[s].bitcast(F32), probT_ps[:, :], ACT.Copy).then_inc(probT_evac, 1)

            def step(t, c):
                n, before = NU * t + c, (c - 1) % NU
                proj, heads, attend = live(n, 0), live(n, 1), live(n, 2)
                if attend:
                    expo(n - 2, c % 2)
                if proj:
                    evacuate(n, c, 0)
                if heads:
                    norm_bank2(n - 1, before)
                if proj:
                    evacuate(n, c, 1)
                if heads:
                    heads_out(n - 1, before, 0)
                if attend:
                    prob_high(n - 2, c % 2)
                if proj:
                    evacuate(n, c, 2)
                if heads:
                    heads_out(n - 1, before, 1)
                if proj:
                    evacuate_values(t, c)
                if heads:
                    heads_out(n - 1, before, 2)
                if proj:
                    roots(n)
                if attend:
                    prob_out(n - 2, c % 2)
                if proj and c == 2 and live(n, -NU):
                    inputs_high(t + 1)

            run_steps(act, step)
            root(2, tw[:, 0, :], tw[:, 1, :], tw[:, 2, :])
            for k in range(4):
                c, half = k // 2, k % 2
                act.wait_ge(xT_done, 4 + k + 1)
                src = wide_ps[k][:, :]
                act.activation(zh[:, c, half * 512:half * 512 + 512], src, ACT.Copy)
                act.activation(zT[:, c, half * 512:half * 512 + 512], src, ACT.Copy).then_inc(xT_evac, 1)
            act.wait_ge(rexp_in, 1)
            act.activation(rt[2], rt[2], ACT.Exp).then_inc(rexp_done, 1)

            def split_hi(n, j):
                act.wait_ge(we_ld[j % 2], 16 * (n // 2 + 1) if isinstance(n, int) else 8 * (n - j % 2) + 16)
                ge(act, down_done, n - 3)
                act.activation(weh[j], wst[j % 2], ACT.Copy, scale=WF_SCALE).then_inc(we_hi, 1)

            def silu(n, j):
                act.wait_ge(up_done, n + 1)
                ge(act, prod_done, n - 1)
                act.activation(hs[j % 2], ups[j % 2][0][:, :], ACT.Silu, scale=1.0 / WF_SCALE)\
                   .then_inc(silu_done, 1)

            def hidden_hi(n, j):
                act.wait_ge(hid_done, n + 1)
                ge(act, down_done, n - 3)
                act.activation(hh[j], hf[j % 2], ACT.Copy).then_inc(hid_hi, 1)

            for n in range(3):
                split_hi(n, n)

            def expert(n, j, ahead=True):
                silu(n, j)
                if ahead:
                    split_hi(n + 3, (j + 3) % 4)
                hidden_hi(n, j)

            for n in range(4):
                expert(n, n)
            with act.Fori(1, NX // 2 - 1) as i:
                for j in range(4):
                    expert(4 * i + j, j)
            for j in range(4):
                expert(2 * NX - 4 + j, j, ahead=(j == 0))

        @block.tensor
        def _(pe):
            def wide_transposes(n0, done):
                for k in range(4):
                    c, half = k // 2, k % 2
                    for j in range(4):
                        t = 4 * half + j
                        mm = pe.transpose(wide_ps[k][:, j * P:(j + 1) * P],
                                          xn[:, t * H + c * P:t * H + c * P + P], idf[:, :])
                    mm.then_inc(done, 1)

            pe.wait_ge(ld_small, 48)
            pe.wait_ge(xn_done, 1)
            wide_transposes(0, xT_done)

            def project(t, c, i):
                kind, b = BANKS[4 * c + i]
                n = NU * t + c
                ge(pe, proj_evac, 4 * n + i - 1)
                ps = proj_ps[i % 2][:, :]
                first = isinstance(t, int) and t == 0
                if kind in ("kx", "vx"):
                    if first:
                        pe.wait_ge(ctx_ready, 1)
                        pe.wait_ge(wkv_ready, 1)
                    o = (G * D if kind == "vx" else 0) + 512 * b
                    parts = [(ctxh, wkvh), (ctxh, wkvl), (ctxl, wkvh)]
                    k = 0
                    for a, w in parts:
                        for ch in range(HC):
                            lhs = a[:, ch, bass.ds(t * P, P)]
                            mm = pe.matmul(ps, lhs, w[:, ch, o:o + 512], start=(k == 0), stop=(k == 5))
                            k += 1
                else:
                    j = XORDER.index(kind)
                    pe.wait_ge(xs_ready, t + 1)
                    if first:
                        pe.wait_ge(ld_w[kind], 16)
                    k = 0
                    for a in (XHf, XLf):
                        for ch in range(HC):
                            lhs = a[:, bass.ds(t * XW + (j * HC + ch) * P, P)]
                            mm = pe.matmul(ps, lhs, wb[kind][:, ch, 512 * b:512 * b + 512],
                                           start=(k == 0), stop=(k == 3))
                            k += 1
                mm.then_inc(proj_done, 1)

            def head_transposes(n, c, i):
                if i < 2:
                    pe.wait_ge(norm_done, 2 * n + i + 1)
                else:
                    pe.wait_ge(norm2_done, n + 1)
                ge(pe, headT_evac, 3 * n + i)
                for h in range(4):
                    if i > 0:
                        dst = headT_ps[:, :].rearrange("p (g b h s) -> p g b h s", g=2, b=2, h=2)\
                            [:, h // 2, :, h % 2, :]
                    else:
                        dst = headT_ps[:, h * P:(h + 1) * P]
                    mm = pe.transpose(dst, raw[c % 2][i][:, h * D:(h + 1) * D], idf[:, :])
                mm.then_inc(headT_done, 1)

            def scores(w, s):
                pe.wait_ge(headT_evac, 3 * w + 3)
                ge(pe, sub_done, w)
                for g in range(4):
                    for b in range(2):
                        mm = pe.matmul(score_ps[:, (2 * g + b) * S:(2 * g + b + 1) * S], qT[:, s, 2 * g + b, :],
                                       kT[:, s, g, b * S:(b + 1) * S], start=True, stop=True)
                mm.then_inc(score_done, 1)

            def prob_transposes(w, s):
                pe.wait_ge(prob_lo, w + 1)
                ge(pe, probT_evac, w)
                ps = probT_ps[:, :].bitcast(F16)
                for g in range(8):
                    mm = pe.transpose(ps[:, g * P:(g + 1) * P], probs[:, s, g * P:(g + 1) * P], idh[:, :])
                mm.then_inc(probT_done, 1)

            def values(w, u):
                pe.wait_ge(probT_evac, w + 1)
                pe.wait_ge(v_lo, w + 1)
                ge(pe, y_done, w)
                pT = probT[u % 2]
                for g in range(4):
                    for b in range(2):
                        rows = slice(b * S, (b + 1) * S)
                        o = pv_ps[b][:, g * P:(g + 1) * P]
                        lo = 512 + g * P
                        vhi, vlo = vh[rows, u, g * D:(g + 1) * D], vl16[rows, u, g * D:(g + 1) * D]
                        pe.matmul(o, vhi, pT[rows, g * P:(g + 1) * P], start=True, stop=False)
                        pe.matmul(o, vhi, pT[rows, lo:lo + P], start=False, stop=False)
                        mm = pe.matmul(o, vlo, pT[rows, g * P:(g + 1) * P], start=False, stop=True)
                mm.then_inc(pv_done, 1)

            def output(w, u, tile):
                pe.wait_ge(catq_done, w + 1)
                if u == 0:
                    ge(pe, res_done, tile)
                for h in range(8):
                    mm = pe.matmul(out_ps[:, 0:H], catq[u % 2][:, h * P:(h + 1) * P], wp[:, 8 * u + h, :],
                                   start=(u == 0 and h == 0), stop=(u == NU - 1 and h == 7))
                mm.then_inc(op_done, 1)

            def step(t, c):
                n, before = NU * t + c, (c - 1) % NU
                proj, heads, attend = live(n, 0), live(n, 1), live(n, 2)
                if attend:
                    scores(n - 2, c % 2)
                if live(n, 4):
                    output(n - 4, c, t - 1)
                if proj:
                    project(t, c, 0)
                if live(n, 3):
                    values(n - 3, (c - 3) % NU)
                if proj:
                    project(t, c, 1)
                if heads:
                    head_transposes(n - 1, before, 0)
                if proj:
                    project(t, c, 2)
                if heads:
                    head_transposes(n - 1, before, 1)
                if proj:
                    project(t, c, 3)
                if heads:
                    head_transposes(n - 1, before, 2)
                if attend:
                    prob_transposes(n - 2, c % 2)

            pe.wait_ge(xT_evac, 4)
            pe.wait_ge(ld_wp, 16)
            pe.wait_ge(idh_done, 1)
            run_steps(pe, step)
            pe.wait_ge(xn_done, 2)
            wide_transposes(4, xT_done)
            pe.wait_ge(xT_evac, 8)
            pe.wait_ge(ld_tail, 32)
            for t in range(NT):
                for c in range(HC):
                    mm = pe.matmul(proj_ps[0][:, t * NE:(t + 1) * NE], zT[:, c, t * P:(t + 1) * P],
                                   rws[:, c, :], start=(c == 0), stop=(c == HC - 1))
            mm.then_inc(logit_done, 1)
            pe.wait_ge(comb_done, 1)
            cps = headT_ps[:, :].bitcast(BF16)
            for t in range(NT):
                mm = pe.transpose(cps[0:NROW, t * P:(t + 1) * P], cbt[:, t, 0:NROW], idb)
            mm.then_inc(combT_done, 1)

            pe.wait_ge(combT_evac, 1)
            pe.wait_ge(zl_done, 4)

            def up(n, e, j, half):
                par = j % 2
                pe.wait_ge(we_lo, n + 1)
                pe.wait_ge(we_hi, n + 1)
                ge(pe, hid_done, n - 1)
                tok = slice(half * 512, half * 512 + 512)
                for wo, ps in ((0, ups[par][0]), (H, ups[par][1])):
                    k = 0
                    for w, z in ((weh[j], zh), (wel[j], zh), (weh[j], zl)):
                        for c in range(HC):
                            pe.matmul(ps[:, :], w[:, wo + c * P:wo + c * P + P], z[:, c, tok],
                                      start=(k == 0), stop=(k == 5))
                            k += 1
                pe.matmul(ups[par][2][:, :], sel_sb[:, e, :] if isinstance(e, int)
                          else sel_sb[:, bass.ds(e, 1), :].rearrange("p a m -> p (a m)"),
                          combT[:, tok], start=True, stop=True).then_inc(up_done, 1)

            def down(n, j, first, last):
                pe.wait_ge(hid_lo, n + 1)
                for i in range(4):
                    ps = pv_ps[i // 2][:, (i % 2) * H:(i % 2) * H + H]
                    ti = slice(i * P, i * P + P)
                    for k, (a, w) in enumerate(((hh, weh), (hl, weh), (hh, wel))):
                        mm = pe.matmul(ps, a[j][:, ti], w[j][:, 2 * H:3 * H],
                                       start=(first and i % 2 == 0 and k == 0), stop=(last and k == 2),
                                       skip_group_check=True)
                mm.then_inc(down_done, 1)

            def expert(n, j):
                m = n + 2
                if m < 2 * NX:
                    up(m, m % NX, m % 4, m // NX)
                if n == NX:
                    pe.wait_ge(y_ready, 4)
                down(n, n % 4, n % NX == 0, n % NX == NX - 1)

            up(0, 0, 0, 0)
            up(1, 1, 1, 0)
            for n in range(4):
                expert(n, n)
            with pe.Fori(1, 4) as i:
                for j in range(4):
                    up(4 * i + j + 2, 4 * i + j + 2, (j + 2) % 4, 0)
                    down(4 * i + j, j, False, False)
            for n in range(16, 20):
                expert(n, n % 4)
            with pe.Fori(5, 8) as i:
                for j in range(4):
                    up(4 * i + j + 2, 4 * i + (j + 2 - NX), (j + 2) % 4, 1)
                    down(4 * i + j, j, False, False)
            for n in range(32, 36):
                expert(n, n % 4)

        @block.vector
        def _(ve):
            links = [0]

            def link(ins):
                links[0] += 1
                ins.then_inc(dchain, 1)
                ve.wait_ge(dchain, links[0])

            def newton(r, v, a, b):
                link(ve.tensor_tensor(a, v, r, ALU.mult))
                link(ve.tensor_tensor(b, a, r, ALU.mult))
                link(ve.tensor_scalar(a, b, -0.5, 1.5, ALU.mult, ALU.add))
                link(ve.tensor_tensor(r, r, a, ALU.mult))

            def row_stats():
                for t in range(NT):
                    ins = ve.bn_stats(tst[:, t, :], xs[:, t * H:(t + 1) * H])
                link(ins)
                for t in range(NT):
                    ins = ve.bn_aggr(tmv[:, t, :], tst[:, t, :])
                link(ins)

            ve.wait_ge(ld_small, 48)
            a0, b0 = COL["in_k"][0], COL["in_qx"][1]
            ve.reciprocal(sinv[:, :], colv[:, a0:b0])
            a0, b0 = COL["smooth"]
            ve.reciprocal(smi[:, :], colv[:, a0:b0])
            for x, h0, h1, scale in ((0, 0, 4, "s_k"), (0, 4, NLH, "s_q"), (1, 4, NLH, "s_qx")):
                ve.tensor_copy(lnW[:, x, h0:h1], col(scale).to_broadcast([P, h1 - h0]))
            link(ve.memset(lnW[:, 1, 0:4], 1.0 / WKV_SCALE))
            ve.memset(lnC[:, 2, :, :], EPS)
            ve.memset(lnC[:, 5, :, :], -0.5)
            link(ve.tensor_scalar(lnC[:, 0, :, :], lnW[:, :, :], 1.0 / D, None, ALU.mult))
            link(ve.tensor_tensor(lnC[:, 0, :, :], lnC[:, 0, :, :], lnW[:, :, :], ALU.mult))
            ve.tensor_scalar(lnC[:, 1, :, :], lnC[:, 0, :, :], D / 4.0, None, ALU.mult)
            ve.tensor_scalar(lnC[:, 3, :, :], lnW[:, :, :], -0.5, None, ALU.mult)
            ve.tensor_scalar(lnC[:, 4, :, :], lnW[:, :, :], 1.5, None, ALU.mult).then_inc(prep_done, 1)
            ve.wait_ge(tanh_done, 1)
            ve.tensor_scalar(gate[:, 0:1], th[:, 0:1], col("s_proj"), None, ALU.mult)
            link(ve.tensor_scalar(gate[:, 1:2], th[:, 1:2], 1.0 / WF_SCALE, None, ALU.mult))
            link(ve.tensor_scalar(gate[:, 2:3], gate[:, 0:1], col("s_pin"), None, ALU.mult))

            ve.tensor_copy(idh[:, :], idf[:, :]).then_inc(idh_done, 1)

            ve.wait_ge(ld_x, 16)
            row_stats()
            var, mean = tmv[:, :, 1], tmv[:, :, 0]
            link(ve.tensor_scalar(tw[:, 0, :], var, EPS, None, ALU.add))
            ve.tensor_scalar(tw[:, 3, :], var, 1.0, None, ALU.mult).then_inc(ln_in, 1)
            ve.wait_ge(ln_root, 1)
            newton(tw[:, 2, :], tw[:, 0, :], tw[:, 4, :], tw[:, 5, :])
            link(ve.tensor_copy(tn[:, 0, :], tw[:, 2, :]))
            link(ve.tensor_tensor(tw[:, 4, :], tn[:, 0, :], tn[:, 0, :], ALU.mult))
            link(ve.tensor_tensor(tw[:, 5, :], tw[:, 4, :], var, ALU.mult))
            link(ve.tensor_scalar(tw[:, 0, :], tw[:, 5, :], EPS, None, ALU.add))
            ve.tensor_scalar(tw[:, 3, :], var, 1.0, None, ALU.mult).then_inc(ln_in, 1)
            ve.wait_ge(ln_root, 2)
            newton(tw[:, 2, :], tw[:, 0, :], tw[:, 4, :], tw[:, 5, :])
            link(ve.tensor_tensor(tn[:, 0, :], tn[:, 0, :], tw[:, 2, :], ALU.mult))
            link(ve.scalar_tensor_tensor(tn[:, 1, :], mean, -1.0, tn[:, 0, :], ALU.mult, ALU.mult))

            def row_norm():
                for t in range(NT):
                    ins = ve.tensor_scalar(xn[:, t * H:(t + 1) * H], xs[:, t * H:(t + 1) * H],
                                           tn[:, 0, t:t + 1], tn[:, 1, t:t + 1], ALU.mult, ALU.add)
                ins.then_inc(xn_done, 1)

            row_norm()

            def to_grid(y, q, sems, n, wait_free=None):
                clip, absolute, mag, big, grid = sems
                ve.tensor_scalar(y, y, FP8_MAX, -FP8_MAX, ALU.min, ALU.max).then_inc(clip, 1)
                ve.wait_ge(clip, n + 1)
                ve.tensor_scalar(ya[:, :].bitcast(U16), y.bitcast(U16), 0x7FFF, None,
                                 ALU.bitwise_and).then_inc(absolute, 1)
                ve.wait_ge(absolute, n + 1)
                ve.tensor_scalar(ym[:, :], ya[:, :], 128.0, 3.0, ALU.mult, ALU.max).then_inc(mag, 1)
                ve.wait_ge(mag, n + 1)
                ve.tensor_tensor(ys[:, :], y, ym[:, :], ALU.add).then_inc(big, 1)
                ve.wait_ge(big, n + 1)
                if wait_free:
                    wait_free()
                ve.tensor_tensor(q, ys[:, :], ym[:, :], ALU.subtract).then_inc(grid, 1)

            def inputs_to_grid(T):
                ve.wait_ge(xin_done, T + 1)
                to_grid(xin[:, :], xin[:, :], (xclip_done, xabs_done, xmag_done, xbig_done, xgrid_done), T)

            inputs_to_grid(0)

            def stats(n, c, i):
                ve.wait_ge(proj_evac, 4 * n + i + 1)
                for h in range(4):
                    ins = ve.bn_stats(st[:, 4 * i + h, :], raw[c % 2][i][:, h * D:(h + 1) * D])
                if i == 2:
                    ins.then_inc(bn_done, 1)

            def norm(n, c, i):
                ve.wait_ge(coef_done, n + 1)
                for h in range(4):
                    r, k = raw[c % 2][i][:, h * D:(h + 1) * D], 4 * i + h
                    ins = ve.tensor_scalar(r, r, cw[:, k:k + 1], cb[:, k:k + 1], ALU.mult, ALU.add)
                ins.then_inc(norm_done, 1)

            def softmax_in(w, s):
                s3 = score_ps[:, :].rearrange("p (g t) -> p g t", t=S)
                ve.wait_ge(score_done, w + 1)
                ve.tensor_reduce(mx[:, :], s3, AX.X, ALU.max).then_inc(max_done, 1)
                ve.wait_ge(max_done, w + 1)
                ge(ve, probn_done, w - 1)
                ve.tensor_tensor(prob[s].rearrange("p (g t) -> p g t", t=S), s3,
                                 mx[:, :].unsqueeze(2).to_broadcast([P, 8, S]),
                                 ALU.subtract).then_inc(sub_done, 1)

            def softmax_sum(w, s):
                ve.wait_ge(exp_done, w + 1)
                ve.tensor_reduce(sm[:, :], prob[s].rearrange("p (g t) -> p g t", t=S), AX.X,
                                 ALU.add).then_inc(sum_done, 1)
                ve.wait_ge(sum_done, w + 1)
                ve.reciprocal(rinv[:, s, :], sm[:, :]).then_inc(rinv_done, 1)

            def quantise(w, u):
                ve.wait_ge(pv_done, w + 1)
                y3 = yv[:, :].rearrange("p (h t) -> p h t", t=P)
                for b in range(2):
                    ins = ve.tensor_tensor(y3[:, :, b * S:(b + 1) * S],
                                           pv_ps[b][:, :].rearrange("p (h t) -> p h t", t=S),
                                           smi[:, 8 * u:8 * u + 8].unsqueeze(2).to_broadcast([P, 8, S]),
                                           ALU.mult)
                ins.then_inc(y_done, 1)
                ve.wait_ge(y_done, w + 1)
                to_grid(yv[:, :], catq[u % 2], (clip_done, abs_done, mag_done, big_done, catq_done), w,
                        lambda: ge(ve, op_done, w - 1))

            def residual(t):
                ve.wait_ge(op_done, NU * (t + 1))
                xt = xs[:, bass.ds(t * H, H)]
                ve.scalar_tensor_tensor(xt, out_ps[:, 0:H], gate[:, 2:3], xt, ALU.mult, ALU.add)\
                  .then_inc(res_done, 1)

            def step(t, c):
                n, before = NU * t + c, (c - 1) % NU
                proj, heads, attend = live(n, 0), live(n, 1), live(n, 2)
                if attend:
                    softmax_in(n - 2, c % 2)
                if heads:
                    norm(n - 1, before, 0)
                if attend:
                    softmax_sum(n - 2, c % 2)
                if heads:
                    norm(n - 1, before, 1)
                if proj:
                    for i in range(3):
                        stats(n, c, i)
                if live(n, 3):
                    quantise(n - 3, (c - 3) % NU)
                if proj and c == 1 and live(n, -NU):
                    inputs_to_grid(t + 1)
                if c == 3 and live(n, NU):
                    residual(t - 1)
                if isinstance(n, int) and n == 0:
                    ve.wait_ge(wkv_hi, 1)
                    ve.scalar_tensor_tensor(wkvl[:, :, :].rearrange("p c t -> p (c t)"), wkv_st, WKV_SCALE,
                                            wkvh[:, :, :].rearrange("p c t -> p (c t)"), ALU.mult,
                                            ALU.subtract).then_inc(wkv_ready, 1)

            run_steps(ve, step)

            ve.wait_ge(res_done, NT)
            row_stats()
            link(ve.tensor_scalar(tw[:, 0, :], var, EPS, None, ALU.add))
            ve.tensor_scalar(tw[:, 3, :], var, 1.0, None, ALU.mult).then_inc(ln_in, 1)
            ve.wait_ge(ln_root, 3)
            newton(tw[:, 2, :], tw[:, 0, :], tw[:, 4, :], tw[:, 5, :])
            link(ve.tensor_copy(tn[:, 0, :], tw[:, 2, :]))
            link(ve.scalar_tensor_tensor(tn[:, 1, :], mean, -1.0, tn[:, 0, :], ALU.mult, ALU.mult))
            row_norm()
            for k in range(4):
                c, half = k // 2, k % 2
                sl = slice(half * 512, half * 512 + 512)
                ve.wait_ge(xT_evac, 4 + k + 1)
                ve.tensor_tensor(zl[:, c, sl], zT[:, c, sl], zh[:, c, sl], ALU.subtract).then_inc(zl_done, 1)
            link(ve.tensor_copy(idb, idf[:, :]))
            ve.wait_ge(logit_done, 1)
            L3 = proj_ps[0][:, 0:NT * NE].rearrange("p (t e) -> p t e", t=NT)
            logits, biased, ex, m1, m2, comb, rem, rem2 = rt
            link(ve.tensor_copy(logits, L3))
            ve.tensor_tensor(biased, logits, rowv[:, 0:NE].unsqueeze(1).to_broadcast([P, NT, NE]), ALU.add)
            link(ve.tensor_reduce(rs8[:, 0, :], logits, AX.X, ALU.max))
            ve.tensor_tensor(ex, logits, rs8[:, 0, :].unsqueeze(2).to_broadcast([P, NT, NE]),
                             ALU.subtract).then_inc(rexp_in, 1)
            for t in range(NT):
                ins = ve.max(m8[:, t, :], biased[:, t, :])
            link(ins)
            for t in range(NT):
                ins = ve.max_index(i8[:, t, :], m8[:, t, :], biased[:, t, :])
            link(ins)
            link(ve.tensor_copy(i8f, i8))
            iota = rowv[:, NE:2 * NE].unsqueeze(1).to_broadcast([P, NT, NE])
            ve.tensor_tensor(m1, iota, i8f[:, :, 0:1].to_broadcast([P, NT, NE]), ALU.is_equal)
            link(ve.tensor_tensor(m2, iota, i8f[:, :, 1:2].to_broadcast([P, NT, NE]), ALU.is_equal))
            link(ve.tensor_tensor(m1, m1, m2, ALU.add))
            ve.wait_ge(rexp_done, 1)
            link(ve.tensor_tensor(m2, ex, m1, ALU.mult))
            link(ve.tensor_reduce(rs8[:, 1, :], m2, AX.X, ALU.add))
            link(ve.reciprocal(rs8[:, 2, :], rs8[:, 1, :]))
            link(ve.tensor_tensor(comb, m2, rs8[:, 2, :].unsqueeze(2).to_broadcast([P, NT, NE]), ALU.mult))
            link(ve.tensor_copy(cbt[:, :, 0:NE], comb))
            link(ve.tensor_tensor(rem, comb, cbt[:, :, 0:NE], ALU.subtract))
            link(ve.tensor_copy(cbt[:, :, NE:2 * NE], rem))
            link(ve.tensor_tensor(rem2, rem, cbt[:, :, NE:2 * NE], ALU.subtract))
            link(ve.tensor_copy(cbt[:, :, 2 * NE:3 * NE], rem2))
            ve.memset(cbt[:, :, 3 * NE:4 * NE], 1.0).then_inc(comb_done, 1)
            ve.wait_ge(combT_done, 1)
            ve.tensor_copy(combT, headT_ps[:, :].bitcast(BF16)[0:NROW, :]).then_inc(combT_evac, 1)

            def split_lo(n, j):
                ve.wait_ge(we_hi, n + 1)
                ve.scalar_tensor_tensor(wel[j], wst[j % 2], WF_SCALE, weh[j], ALU.mult,
                                        ALU.subtract).then_inc(we_lo, 1)

            def hidden(n, j):
                par = j % 2
                ve.wait_ge(silu_done, n + 1)
                ve.scalar_tensor_tensor(ht[par], ups[par][1][:, :], 1.0 / WF_SCALE, hs[par], ALU.mult,
                                        ALU.mult).then_inc(prod_done, 1)
                ve.wait_ge(prod_done, n + 1)
                ge(ve, hid_lo, n - 1)
                ge(ve, hid_hi, n - 1)
                ve.tensor_tensor(hf[par], ht[par], ups[par][2][:, :], ALU.mult).then_inc(hid_done, 1)

            def results(half):
                ve.wait_ge(down_done, NX * (half + 1))
                for j in range(4):
                    t = 4 * half + j
                    ve.scalar_tensor_tensor(yo[t], pv_ps[j // 2][:, (j % 2) * H:(j % 2) * H + H],
                                            gate[:, 1:2], xs[:, t * H:(t + 1) * H], ALU.mult,
                                            ALU.add).then_inc(y_ready, 1)

            for n in range(3):
                split_lo(n, n)

            def expert(n, j, ahead=True):
                hidden(n, j)
                if ahead:
                    split_lo(n + 3, (j + 3) % 4)

            for n in range(4):
                expert(n, n)
            with ve.Fori(1, 4) as i:
                for j in range(4):
                    expert(4 * i + j, j)
            for n in range(16, 20):
                if n == NX + 1:
                    results(0)
                expert(n, n % 4)
            with ve.Fori(5, 8) as i:
                for j in range(4):
                    expert(4 * i + j, j)
            for n in range(32, 36):
                expert(n, n % 4, ahead=(n == 32))
            results(1)


def kernel(**inputs):
    import concourse.bacc as bacc
    from concourse.bass_utils import run_bass_kernel_spmd as run

    v = {k: np.asarray(a) for k, a in inputs.items()}
    at = {k[len("L0_xattn_"):]: a for k, a in v.items() if k.startswith("L0_xattn_")}
    ff = {k[len("L0_ffn_"):]: a for k, a in v.items() if k.startswith("L0_ffn_")}

    def per_row(a):
        return np.ascontiguousarray(a.reshape(-1, P).T)

    def everywhere(a):
        return np.broadcast_to(a.reshape(1, 1), (P, 1))

    cols = np.concatenate(
        [per_row(at[k]) for k in ("ln_w", "ln_b", "k_in_scale", "q_in_scale", "v_in_scale", "qx_in_scale",
                                  "qln_w", "kln_w", "qxln_w", "kxln_w", "qln_b", "kln_b", "qxln_b", "kxln_b",
                                  "proj_smooth")]
        + [everywhere(a) for a in (at["wq_scale"], at["wk_scale"], at["wqx_scale"], at["wv_scale"],
                                   at["proj_w_scale"], at["proj_in_scale"], v["g_xattn"], v["g_ffn"])], axis=1)
    rowc = np.concatenate([np.broadcast_to(ff["router_bias"][None, :], (P, NE)),
                           np.broadcast_to(np.arange(NE, dtype=np.float32)[None, :], (P, NE))], axis=1)
    sel = np.zeros((NROW, NX, P), np.float32)
    for e in range(NX):
        for r in ((e, NE + e, 2 * NE + e) if e < NE else (3 * NE,)):
            sel[r, e, :] = 1.0

    def up(we, ws):
        a = np.concatenate([we.transpose(1, 0, 2).reshape(H, NE * FE), ws[0]], axis=1)
        return a.reshape(HC, P, NX, FE).transpose(2, 1, 0, 3).reshape(NX, P, HC * FE)

    wffn = np.concatenate([up(ff["Wu"], ff["Su"]), up(ff["Wg"], ff["Sg"]),
                           np.concatenate([ff["Wd"], ff["Sd"][0].reshape(NSH, FE, H)], axis=0)], axis=2)
    arrays = {
        "x": v["x"].reshape(TOK, H), "cols": cols, "rowc": rowc, "ident": np.eye(P, dtype=np.float32),
        "sel": sel.reshape(NROW, NX * P), "ctxT": v["ctx_2048"].reshape(TOK, H).T,
        "wkvT": at["w_kv_x"].T, "wqT": at["wq"].T, "wkT": at["wk"].T, "wvT": at["wv"].T,
        "wqxT": at["wqx"].T, "wpT": at["wproj"].T, "rwT": ff["router_w"].T, "wffn": wffn,
    }
    nc = bacc.Bacc("TRN2", target_bir_lowering=False, num_devices=1)
    feed, args = {}, []
    for name, a in arrays.items():
        a = np.ascontiguousarray(a)
        feed["in_" + name] = a
        args.append(nc.dram_tensor("in_" + name, a.shape, mybir.dt.from_np(a.dtype), kind="ExternalInput").ap())
    args.append(nc.dram_tensor("out_y", (TOK, H), F32, kind="ExternalOutput").ap())
    build(nc, *args)
    r = run(nc, [feed], core_ids=[0])
    return r.results[0]["out_y"].reshape(NB, S, H)
```

```python
from contextlib import ExitStack

import numpy as np

import concourse.bass as bass
from concourse import mybir

F32 = mybir.dt.float32
F16 = mybir.dt.float16
BF16 = mybir.dt.bfloat16
U16 = mybir.dt.uint16
U32 = mybir.dt.uint32
ALU = mybir.AluOpType
ACT = mybir.ActivationFunctionType
AX = mybir.AxisListType

P = 128
NB, S, H = 16, 64, 256
TOK = NB * S
NT = TOK // P
HC = H // P
D = 128
NH, G = 16, 8
NE, TOPK, FE = 16, 2, 128
NSH = 2
NX = NE + NSH
EPS = 1e-5
FP8_MAX = 448.0
SCORE_SCALE = 1.0 / float(np.sqrt(D))
WKV_SCALE = 64.0
WF_SCALE = 16.0
NROW = 3 * NE + 1

COL = {}
_n = 0
for _name, _w in (("lnw", HC), ("lnb", HC), ("in_k", HC), ("in_q", HC), ("in_v", HC), ("in_qx", HC),
                  ("qw", 1), ("kw", 1), ("qxw", 1), ("kxw", 1), ("qb", 1), ("kb", 1), ("qxb", 1), ("kxb", 1),
                  ("smooth", 2 * NH), ("s_q", 1), ("s_k", 1), ("s_qx", 1), ("s_v", 1),
                  ("s_proj", 1), ("s_pin", 1), ("g_x", 1), ("g_f", 1)):
    COL[_name] = (_n, _n + _w)
    _n += _w
NCOL = _n

BANKS = [("k", 0), ("q", 0), ("q", 1), ("v", 0),
         ("k", 1), ("q", 2), ("q", 3), ("v", 1),
         ("kx", 0), ("qx", 0), ("qx", 1), ("vx", 0),
         ("kx", 1), ("qx", 2), ("qx", 3), ("vx", 1)]
XORDER = ("k", "q", "v", "qx")


def ge(eng, sem, value):
    if isinstance(value, int) and value <= 0:
        return
    eng.wait_ge(sem, value)


def live(n, back):
    return not isinstance(n, int) or 0 <= n - back < 4 * NT


def run_steps(eng, step, between={}):
    for c in range(4):
        step(0, c)
    with eng.Fori(1, NT - 1) as t:
        for c in range(4):
            step(t, c)
    for n in range(4 * (NT - 1), 4 * NT + 4):
        between.get(n, lambda: None)()
        step(n // 4, n % 4)


def build(nc, x, cols, rowc, ident, sel, ctxT, wkvT, wqT, wkT, wvT, wqxT, wpT, rwT, wffn, out):
    ctx = ExitStack()
    with ctx:
        def sb(name, shape, dt):
            return ctx.enter_context(nc.sbuf_tensor(name, shape, dt))

        def bank(name):
            return ctx.enter_context(nc.psum_tensor(name, [P, 512], F32))

        def sem(name):
            return ctx.enter_context(nc.semaphore(name))

        NU = 4
        NHT = NT // 2
        XW = 4 * HC * P

        proj_ps = [bank("proj_ps0"), bank("proj_ps1")]
        headT_ps = bank("headT_ps")
        probT_ps = bank("probT_ps")
        score_ps = bank("score_ps")
        pv_ps = [bank("pv_ps0"), bank("pv_ps1")]
        out_ps = bank("out_ps")
        wide_ps = [score_ps, out_ps, pv_ps[0], pv_ps[1]]

        xs = sb("xs", [P, NT * H], F32)
        colv = sb("colv", [P, NCOL], F32)
        rowv = sb("rowv", [P, 2 * NE], F32)
        idf = sb("idf", [P, P], F32)
        XHf = sb("XH", [P, NT * XW], F16)
        XLf = sb("XL", [P, NT * XW], F16)
        ctxh = sb("ctxh", [P, HC, TOK], F16)
        ctxl = sb("ctxl", [P, HC, TOK], F16)
        wkvh = sb("wkvh", [P, HC, 2 * G * D], F16)
        wkvl = sb("wkvl", [P, HC, 2 * G * D], F16)
        wb = {"q": sb("wq_sb", [P, HC, NH * D], BF16), "k": sb("wk_sb", [P, HC, G * D], BF16),
              "v": sb("wv_sb", [P, HC, G * D], BF16), "qx": sb("wqx_sb", [P, HC, NH * D], BF16)}
        wp = sb("wp_sb", [P, 2 * NH, H], BF16)
        rot = sb("rot", [P, 6, 512], F32)
        raw = [[rot[:, 3 * i + b, :] for b in range(3)] for i in range(2)]
        xn = rot[:, 0:4, :].rearrange("p a b -> p (a b)")
        xT = sb("xT", [P, HC, TOK], F32)
        xin = sb("xin", [P, XW], BF16)
        xpr = sb("xpr", [P, XW], F32)
        xn2 = [xpr[:, :], rot[:, 3:5, :].rearrange("p a b -> p (a b)")]
        qT = sb("qT", [P, 2, 8, P], F32)
        kT = sb("kT", [P, 2, 4, P], F32)
        vf = sb("vf", [P, 2, 512], F32)
        vh = sb("vh", [P, NU, 512], F16)
        vl16 = sb("vl16", [P, NU, 512], F16)
        wkv_stage = sb("wkv_stage", [P, 4096], F32)
        reg1 = sb("reg1", [P, 2048], F32)
        reg2 = sb("reg2", [P, 2048], F32)
        prob = [reg1[:, 512 * i:512 * i + 512] for i in range(2)]
        probn = [reg1[:, 1024 + 512 * i:1536 + 512 * i] for i in range(2)]
        ctx_st = reg2[:, :]
        probT = [reg2[:, 512 * i:512 * i + 512].bitcast(F16) for i in range(2)]
        catq = [reg2[:, 1024 + 512 * i:1536 + 512 * i].bitcast(BF16) for i in range(2)]
        wkv_st = wkv_stage[:, :]
        probs = sb("probs", [P, 2, 1024], F16)
        idh = sb("idh", [P, P], F16)
        yv = sb("yv", [P, 1024], BF16)
        ya = sb("ya", [P, 1024], BF16)
        ym = sb("ym", [P, 1024], F16)
        ys = sb("ys", [P, 1024], F16)
        mx = sb("mx", [P, 8], F32)
        sm = sb("sm", [P, 8], F32)
        rinv = sb("rinv", [P, 2, 8], F32)
        NLH = 12
        st = sb("st", [P, NLH, 6], F32)
        mean2 = sb("mean2", [P, NLH], F32)
        vw = sb("vw", [P, 6, NLH], F32)
        va = sb("va", [P, NLH], F32)
        vl = sb("vl", [P, NLH], F32)
        r0 = sb("r0", [P, NLH], F32)
        nw = sb("nw", [P, 5, NLH], F32)
        cw = sb("cw", [P, NLH], F32)
        cb = sb("cb", [P, NLH], F32)
        sinv = sb("sinv", [P, 4 * HC], F32)
        smi = sb("smi", [P, 2 * NH], F32)
        lnC = sb("lnC", [P, 6, 2, NLH], F32)
        lnW = sb("lnW", [P, 2, NLH], F32)
        th = sb("th", [P, 2], F32)
        gate = sb("gate", [P, 3], F32)
        tst = sb("tst", [P, NT, 6], F32)
        tmv = sb("tmv", [P, NT, 2], F32)
        tw = sb("tw", [P, 8, NT], F32)
        tn = sb("tn", [P, 2, NT], F32)

        NS = 4
        zh = XHf[:, 0:2048].rearrange("p (c t) -> p c t", c=HC)
        zl = XHf[:, 2048:4096].rearrange("p (c t) -> p c t", c=HC)
        zT = XLf[:, 0:4096].bitcast(F32).rearrange("p (c t) -> p c t", c=HC)
        WE = 3 * H
        wst = [XLf[:, 4096 + 2 * WE * i:4096 + 2 * WE * (i + 1)].bitcast(F32) for i in range(2)]
        weh, wel = [[a[:, :, :].rearrange("p c o -> p (c o)")[:, WE * i:WE * (i + 1)] for i in range(NS)]
                    for a in (wkvh, wkvl)]
        hs = [wkv_stage[:, 512 * i:512 + 512 * i] for i in range(2)]
        ht = [wkv_stage[:, 1024 + 512 * i:1536 + 512 * i] for i in range(2)]
        hf = [XHf[:, 4096 + 1024 * i:5120 + 1024 * i].bitcast(F32) for i in range(2)]
        hh = [XHf[:, 6144 + 512 * i:6656 + 512 * i] for i in range(NS)]
        hl = [reg1[:, 256 * i:256 * i + 256].bitcast(F16) for i in range(NS)]
        yo = [wkv_stage[:, 2048 + 256 * i:2304 + 256 * i] for i in range(NT)]
        tail = wb["qx"][:, :, :].rearrange("p c o -> p (c o)").bitcast(F32)
        sel_sb = tail[0:NROW, 0:NX * P // 2].bitcast(BF16).rearrange("p (e m) -> p e m", e=NX)
        combT = tail[0:NROW, 1152:1664].bitcast(BF16)
        idb = tail[:, 1664:1728].bitcast(BF16)
        rws = tail[:, 1728:1760].rearrange("p (c e) -> p c e", c=HC)
        NTE = NT * NE
        ctxhf, ctxlf = [a[:, :, :].rearrange("p c t -> p (c t)").bitcast(F32) for a in (ctxh, ctxl)]
        rt = [ctxhf[:, NTE * i:NTE * (i + 1)].rearrange("p (t e) -> p t e", t=NT) for i in range(8)]
        m8 = ctxlf[:, 0:64].rearrange("p (t k) -> p t k", t=NT)
        i8 = ctxlf[:, 64:128].bitcast(U32).rearrange("p (t k) -> p t k", t=NT)
        i8f = ctxlf[:, 128:192].rearrange("p (t k) -> p t k", t=NT)
        rs8 = ctxlf[:, 192:216].rearrange("p (a t) -> p a t", a=3)
        cbt = ctxlf[:, 256:256 + NT * 32].bitcast(BF16).rearrange("p (t e) -> p t e", t=NT)

        def col(name, c=0):
            a = COL[name][0] + c
            return colv[:, a:a + 1]

        ld_x = [sem("ld_x0"), sem("ld_x1")]
        ld_cols = sem("ld_cols")
        ld_small = sem("ld_small")
        ld_ctx = sem("ld_ctx")
        ld_wkv = sem("ld_wkv")
        ld_w = {k: sem("ld_w" + k) for k in ("k", "q", "v", "qx")}
        ld_wp = sem("ld_wp")
        ld_tail = sem("ld_tail")
        prep_done = sem("prep_done")
        tanh_done = sem("tanh_done")
        ln_in = sem("ln_in")
        ln_mid = sem("ln_mid")
        ln_root = sem("ln_root")
        dchain = sem("dchain")
        xn_done = sem("xn_done")
        xT_done = sem("xT_done")
        xT_evac = sem("xT_evac")
        xin_done = sem("xin_done")
        xclip_done = sem("xclip_done")
        xabs_done = sem("xabs_done")
        xmag_done = sem("xmag_done")
        xbig_done = sem("xbig_done")
        xgrid_done = sem("xgrid_done")
        xpr_done = sem("xpr_done")
        xhi_done = sem("xhi_done")
        xs_ready = sem("xs_ready")
        ctx_hi = sem("ctx_hi")
        ctx_ready = sem("ctx_ready")
        wkv_hi = sem("wkv_hi")
        wkv_ready = sem("wkv_ready")
        proj_done = sem("proj_done")
        proj_evac = sem("proj_evac")
        bn_done = sem("bn_done")
        achain = sem("achain")
        var_done = sem("var_done")
        log_done = sem("log_done")
        root_done = sem("root_done")
        nchain = sem("nchain")
        coef_done = sem("coef_done")
        norm0_done = sem("norm0_done")
        norm1_done = sem("norm1_done")
        scale2_done = sem("scale2_done")
        norm2_done = sem("norm2_done")
        headT_done = sem("headT_done")
        headT_evac = sem("headT_evac")
        score_done = sem("score_done")
        max_done = sem("max_done")
        sub_done = sem("sub_done")
        exp_done = sem("exp_done")
        sum_done = sem("sum_done")
        rinv_done = sem("rinv_done")
        probn_done = sem("probn_done")
        prob_hi = sem("prob_hi")
        prob_lo = sem("prob_lo")
        v_hi = sem("v_hi")
        v_lo = sem("v_lo")
        idh_done = sem("idh_done")
        probT_done = sem("probT_done")
        probT_evac = sem("probT_evac")
        pv_done = sem("pv_done")
        y_done = sem("y_done")
        clip_done = sem("clip_done")
        abs_done = sem("abs_done")
        mag_done = sem("mag_done")
        big_done = sem("big_done")
        catq_done = sem("catq_done")
        op_done = sem("op_done")
        res_done = sem("res_done")
        z_done = sem("z_done")
        z_evac = sem("z_evac")
        zl_done = sem("zl_done")
        logit_done = sem("logit_done")
        rexp_in = sem("rexp_in")
        rexp_done = sem("rexp_done")
        comb_done = sem("comb_done")
        combT_done = sem("combT_done")
        combT_evac = sem("combT_evac")
        we_ld = [sem("we_ld0"), sem("we_ld1")]
        we_hi = sem("we_hi")
        we_lo = sem("we_lo")
        up_done = sem("up_done")
        comb_rows = sem("comb_rows")
        silu_done = sem("silu_done")
        prod_done = sem("prod_done")
        hid_done = sem("hid_done")
        hid_hi = sem("hid_hi")
        hid_lo = sem("hid_lo")
        down_done = sem("down_done")
        y_ready = sem("y_ready")
        stored = sem("stored")

        ups = [(proj_ps[0], headT_ps), (proj_ps[1], probT_ps)]
        comb_ps = score_ps
        z_ps = [(proj_ps[0], proj_ps[1]), (out_ps, out_ps)]
        logit_ps = [proj_ps[1], out_ps]
        combT_ps = [proj_ps[1], out_ps]

        block = ctx.enter_context(nc.Block())
        @block.sync
        def _(sp):
            for half in range(2):
                sp.dma_start(xs[:, half * NHT * H:(half + 1) * NHT * H].rearrange("p (t d) -> p t d", t=NHT),
                             x[half * NHT * P:(half + 1) * NHT * P, :].rearrange("(t p) d -> p t d", p=P))\
                  .then_inc(ld_x[half], 16)
            sp.wait_ge(ld_w["k"], 16)
            sp.dma_start(ctx_st.rearrange("p (c t) -> p c t", c=HC),
                         ctxT.rearrange("(c p) t -> p c t", p=P)).then_inc(ld_ctx, 16)
            sp.wait_ge(ld_w["q"], 16)
            sp.dma_start(wkv_st.rearrange("p (c t) -> p c t", c=HC),
                         wkvT.rearrange("(c p) t -> p c t", p=P)).then_inc(ld_wkv, 16)
            sp.wait_ge(proj_done, 4 * NU * NT)

            def load(e, n, par):
                ge(sp, we_lo, n - 1)
                ge(sp, we_hi, n - 1)
                sp.dma_start(wst[par], wffn[bass.ds(e, 1), :, :].rearrange("a p n -> p (a n)")
                             if not isinstance(e, int) else wffn[e, :, :]).then_inc(we_ld[par], 16)

            load(0, 0, 0)
            load(1, 1, 1)
            with sp.Fori(1, NX // 2) as i:
                load(2 * i, 2 * i, 0)
                load(2 * i + 1, 2 * i + 1, 1)
            with sp.Fori(0, NX // 2) as i:
                load(2 * i, NX + 2 * i, 0)
                load(2 * i + 1, NX + 2 * i + 1, 1)
            for t in range(NT):
                sp.wait_ge(y_ready, t + 1)
                sp.dma_start(out[t * P:(t + 1) * P, :], yo[t]).then_inc(stored, 16)
            sp.wait_ge(stored, 16 * NT)

        @block.gpsimd
        def _(gp):
            for k, w in (("k", wkT), ("q", wqT), ("v", wvT), ("qx", wqxT)):
                gp.dma_start(wb[k][:, :, :], w.rearrange("(c p) o -> p c o", p=P)).then_inc(ld_w[k], 16)
            gp.dma_start(wp[:, :, :], wpT.rearrange("(h p) o -> p h o", p=P)).then_inc(ld_wp, 16)

            def tile_of(buf, T):
                return buf[:, bass.ds(T * XW, XW)]

            def inputs_over_scale(T):
                gp.wait_ge(xT_evac, 4)
                ge(gp, xpr_done, T)
                gp.tensor_tensor(xin[:, :].rearrange("p (j c t) -> p j c t", j=4, c=HC),
                                 xT[:, :, bass.ds(T * P, P)].unsqueeze(1).to_broadcast([P, 4, HC, P]),
                                 sinv[:, :].rearrange("p (j c) -> p j c", j=4).unsqueeze(3)
                                 .to_broadcast([P, 4, HC, P]), ALU.mult).then_inc(xin_done, 1)

            def inputs_times_scale(T):
                gp.wait_ge(xgrid_done, T + 1)
                ge(gp, xs_ready, T)
                a0 = COL["in_k"][0]
                gp.tensor_tensor(xpr[:, :].rearrange("p (n t) -> p n t", t=P),
                                 xin[:, :].rearrange("p (n t) -> p n t", t=P),
                                 colv[:, a0:a0 + 4 * HC].unsqueeze(2).to_broadcast([P, 4 * HC, P]),
                                 ALU.mult).then_inc(xpr_done, 1)

            def inputs_low(T):
                gp.wait_ge(xhi_done, T + 1)
                gp.tensor_tensor(tile_of(XLf, T), xpr[:, :], tile_of(XHf, T),
                                 ALU.subtract).then_inc(xs_ready, 1)

            def context_low():
                gp.wait_ge(ctx_hi, 1)
                gp.tensor_tensor(ctxl[:, :, :].rearrange("p c t -> p (c t)"), ctx_st,
                                 ctxh[:, :, :].rearrange("p c t -> p (c t)"), ALU.subtract)\
                  .then_inc(ctx_ready, 1)

            gp.wait_ge(prep_done, 1)

            def chained(sem, ins, count):
                ins.then_inc(sem, 1)
                gp.wait_ge(sem, count)

            def variance(n, x):
                gp.wait_ge(bn_done, n + 1)
                ge(gp, coef_done, n)
                even, odd = st[:, :, 1], st[:, :, 4]
                gp.tensor_tensor(mean2[:, :], even, odd, ALU.add)
                gp.tensor_tensor(vw[:, 0, :], st[:, :, 2], st[:, :, 5], ALU.add)
                chained(achain, gp.tensor_tensor(vw[:, 1, :], even, odd, ALU.subtract), 4 * n + 1)
                gp.tensor_tensor(vw[:, 3, :], vw[:, 0, :], lnC[:, 0, x, :], ALU.mult)
                chained(achain, gp.tensor_tensor(vw[:, 2, :], vw[:, 1, :], vw[:, 1, :], ALU.mult), 4 * n + 2)
                chained(achain, gp.tensor_tensor(vw[:, 4, :], vw[:, 2, :], lnC[:, 1, x, :], ALU.mult),
                        4 * n + 3)
                chained(achain, gp.tensor_tensor(vw[:, 5, :], vw[:, 3, :], vw[:, 4, :], ALU.add), 4 * n + 4)
                gp.tensor_tensor(va[:, :], vw[:, 5, :], lnC[:, 2, x, :], ALU.add).then_inc(var_done, 1)

            def coefficients(n, x):
                gp.wait_ge(root_done, n + 1)
                chained(nchain, gp.tensor_tensor(nw[:, 0, :], va[:, :], r0[:, :], ALU.mult), 5 * n + 1)
                chained(nchain, gp.tensor_tensor(nw[:, 1, :], nw[:, 0, :], r0[:, :], ALU.mult), 5 * n + 2)
                chained(nchain, gp.tensor_tensor(nw[:, 2, :], nw[:, 1, :], lnC[:, 3, x, :], ALU.mult),
                        5 * n + 3)
                gp.tensor_tensor(nw[:, 4, :], mean2[:, :], lnC[:, 5, x, :], ALU.mult)
                chained(nchain, gp.tensor_tensor(nw[:, 3, :], nw[:, 2, :], lnC[:, 4, x, :], ALU.add),
                        5 * n + 4)
                ge(gp, norm0_done, n)
                ge(gp, norm1_done, n)
                ge(gp, norm2_done, n)
                chained(nchain, gp.tensor_tensor(cw[:, :], nw[:, 3, :], r0[:, :], ALU.mult), 5 * n + 5)
                gp.tensor_tensor(cb[:, :], nw[:, 4, :], cw[:, :], ALU.mult).then_inc(coef_done, 1)

            def norm_bank2(n, c):
                r = raw[c % 2][2].rearrange("p (h d) -> p h d", d=D)
                gp.wait_ge(coef_done, n + 1)
                gp.tensor_tensor(r, r, cw[:, 8:12].unsqueeze(2).to_broadcast([P, 4, D]), ALU.mult)\
                  .then_inc(scale2_done, 1)
                gp.wait_ge(scale2_done, n + 1)
                gp.tensor_tensor(r, r, cb[:, 8:12].unsqueeze(2).to_broadcast([P, 4, D]), ALU.add)\
                  .then_inc(norm2_done, 1)

            def normalise(w, s):
                gp.wait_ge(rinv_done, w + 1)
                ge(gp, prob_lo, w - 1)
                gp.tensor_tensor(probn[s].rearrange("p (g t) -> p g t", t=S),
                                 prob[s].rearrange("p (g t) -> p g t", t=S),
                                 rinv[:, s, :].unsqueeze(2).to_broadcast([P, 8, S]),
                                 ALU.mult).then_inc(probn_done, 1)

            def prob_low(w, s):
                gp.wait_ge(prob_hi, w + 1)
                gp.tensor_tensor(probs[:, s, 512:1024], probn[s], probs[:, s, 0:512],
                                 ALU.subtract).then_inc(prob_lo, 1)

            def value_low(n, c):
                gp.wait_ge(v_hi, n + 1)
                gp.tensor_tensor(vl16[:, c, :], vf[:, c % 2, :], vh[:, c, :], ALU.subtract).then_inc(v_lo, 1)

            def split_inputs(n, t, c):
                if c == 0 and live(n, -NU):
                    inputs_over_scale(t + 1)
                if c == 1 and live(n, -NU):
                    inputs_times_scale(t + 1)
                if c == 2 and live(n, -NU):
                    inputs_low(t + 1)

            def step(t, c):
                n = NU * t + c
                proj, attend = live(n, 0), live(n, 2)
                if attend:
                    normalise(n - 2, c % 2)
                    prob_low(n - 2, c % 2)
                if proj:
                    variance(n, c // 2)
                    value_low(n, c)
                    coefficients(n, c // 2)
                    split_inputs(n, t, c)
                    norm_bank2(n, c)
                if isinstance(n, int) and n == 0:
                    context_low()

            def load_tail():
                gp.wait_ge(proj_done, 4 * NU * NT)
                gp.dma_start(tail[0:NROW, 0:NX * P // 2].bitcast(BF16), sel).then_inc(ld_tail, 16)
                gp.dma_start(rws, rwT.rearrange("(c p) e -> p c e", p=P)).then_inc(ld_tail, 16)

            run_steps(gp, step, {NU * NT: load_tail})
            def low(n, j):
                gp.wait_ge(hid_hi, n + 1)
                ge(gp, down_done, n - 3)
                gp.tensor_tensor(hl[j % 4], hf[j % 2], hh[j % 4], ALU.subtract).then_inc(hid_lo, 1)

            for n in range(4):
                low(n, n)
            with gp.Fori(1, NX // 2) as i:
                for j in range(4):
                    low(4 * i + j, j)

        @block.scalar
        def _(act):
            act.dma_start(colv[:, :], cols).then_inc(ld_cols, 16)
            act.dma_start(idf[:, :], ident).then_inc(ld_small, 16)
            act.dma_start(rowv[:, :], rowc).then_inc(ld_small, 16)
            act.wait_ge(ld_cols, 16)
            a = COL["g_x"][0]
            act.activation(th[:, :], colv[:, a:a + 2], ACT.Tanh).then_inc(tanh_done, 1)

            act.preload_act_table_set("natural_log_exp_and_others")

            def root(n, src, mid, dst):
                act.wait_ge(ln_in, n + 1)
                act.activation(mid, src, ACT.Ln).then_inc(ln_mid, 1)
                act.wait_ge(ln_mid, n + 1)
                act.activation(dst, mid, ACT.Exp, scale=-0.5).then_inc(ln_root, 1)

            root(0, tw[:, 0, :], tw[:, 1, :], tw[:, 2, :])
            root(1, tw[:, 0, :], tw[:, 1, :], tw[:, 2, :])
            for k in range(4):
                half, c = k // HC, k % HC
                act.wait_ge(xT_done, k + 1)
                act.activation(xT[:, c, half * 512:half * 512 + 512], wide_ps[k][:, :], ACT.Identity,
                               scale=col("lnw", c), bias=col("lnb", c)).then_inc(xT_evac, 1)

            def context_weights_high():
                act.wait_ge(ld_wkv, 16)
                act.activation(wkvh[:, :, :].rearrange("p c t -> p (c t)"), wkv_st, ACT.Copy,
                               scale=WKV_SCALE).then_inc(wkv_hi, 1)

            def inputs_high(T):
                act.wait_ge(xpr_done, T + 1)
                act.activation(XHf[:, bass.ds(T * XW, XW)], xpr[:, :], ACT.Copy).then_inc(xhi_done, 1)

            inputs_high(0)

            def evacuate(n, c, i):
                act.wait_ge(proj_done, 4 * n + i + 1)
                ge(act, headT_done, 3 * (n - 2) + i + 1)
                act.activation(raw[c % 2][i], proj_ps[i % 2][:, :], ACT.Copy).then_inc(proj_evac, 1)

            def evacuate_values(t, c):
                n = NU * t + c
                act.wait_ge(proj_done, 4 * n + 4)
                ge(act, v_lo, n - 1)
                scale = col("s_v") if c < 2 else 1.0 / WKV_SCALE
                act.activation(vf[:, c % 2, :], proj_ps[1][:, :], ACT.Copy, scale=scale).then_inc(proj_evac, 1)
                act.wait_ge(proj_evac, 4 * n + 4)
                ge(act, pv_done, n - 3)
                act.activation(vh[:, c, :], vf[:, c % 2, :], ACT.Copy).then_inc(v_hi, 1)

            def roots(n):
                act.wait_ge(var_done, n + 1)
                act.activation(vl[:, :], va[:, :], ACT.Ln).then_inc(log_done, 1)
                act.wait_ge(log_done, n + 1)
                act.activation(r0[:, :], vl[:, :], ACT.Exp, scale=-0.5).then_inc(root_done, 1)

            def norm_bank0(n, c):
                act.wait_ge(coef_done, n + 1)
                for h in range(4):
                    r = raw[c % 2][0][:, h * D:(h + 1) * D]
                    ins = act.activation(r, r, ACT.Identity, scale=cw[:, h:h + 1], bias=cb[:, h:h + 1])
                ins.then_inc(norm0_done, 1)

            def heads_out(n, c, i):
                kind, b = BANKS[4 * c + i]
                act.wait_ge(headT_done, 3 * n + i + 1)
                ge(act, score_done, n - 1)
                if kind in ("q", "qx"):
                    dst = qT[:, c % 2, 4 * (b % 2):4 * (b % 2) + 4, :]
                else:
                    dst = kT[:, c % 2, :, :]
                act.activation(dst, headT_ps[:, :].rearrange("p (h t) -> p h t", h=4), ACT.Identity,
                               scale=col(kind + "w"), bias=col(kind + "b")).then_inc(headT_evac, 1)

            def expo(w, s):
                act.wait_ge(sub_done, w + 1)
                act.activation(prob[s], prob[s], ACT.Exp, scale=SCORE_SCALE).then_inc(exp_done, 1)

            def prob_high(w, s):
                act.wait_ge(probn_done, w + 1)
                ge(act, probT_done, w - 1)
                act.activation(probs[:, s, 0:512], probn[s], ACT.Copy).then_inc(prob_hi, 1)

            def prob_out(w, s):
                act.wait_ge(probT_done, w + 1)
                ge(act, pv_done, w - 1)
                act.activation(probT[s].bitcast(F32), probT_ps[:, :], ACT.Copy).then_inc(probT_evac, 1)

            def step(t, c):
                n, before = NU * t + c, (c - 1) % NU
                proj, heads, attend = live(n, 0), live(n, 1), live(n, 2)
                if proj:
                    evacuate(n, c, 0)
                if attend:
                    expo(n - 2, c % 2)
                if heads:
                    norm_bank0(n - 1, before)
                if proj:
                    evacuate(n, c, 1)
                    evacuate(n, c, 2)
                if heads:
                    heads_out(n - 1, before, 0)
                if attend:
                    prob_high(n - 2, c % 2)
                if heads:
                    heads_out(n - 1, before, 1)
                if proj:
                    evacuate_values(t, c)
                if heads:
                    heads_out(n - 1, before, 2)
                if attend:
                    prob_out(n - 2, c % 2)
                if proj:
                    roots(n)
                if isinstance(n, int) and n == 0:
                    context_weights_high()
                if proj and c == 2 and live(n, -NU):
                    inputs_high(t + 1)

            def z_out(half, c):
                act.wait_ge(z_done, HC * half + c + 1)
                dst = slice(half * 512, half * 512 + 512)
                act.activation(zh[:, c, dst], z_ps[half][c][:, :], ACT.Copy)
                act.activation(zT[:, c, dst], z_ps[half][c][:, :], ACT.Copy).then_inc(z_evac, 1)

            def router_exp(half):
                act.wait_ge(rexp_in, half + 1)
                ex = rt[2][:, NHT * half:NHT * half + NHT, :]
                act.activation(ex, ex, ACT.Exp).then_inc(rexp_done, 1)

            def row_root(half):
                r = slice(NHT * half, NHT * half + NHT)
                root(2 + half, tw[:, 0, r], tw[:, 1, r], tw[:, 2, r])

            def split_hi(n, j):
                act.wait_ge(we_ld[j % 2], 16 * (n // 2 + 1) if isinstance(n, int) else 8 * (n - j % 2) + 16)
                ge(act, down_done, n - 3)
                act.activation(weh[j], wst[j % 2], ACT.Copy, scale=WF_SCALE).then_inc(we_hi, 1)

            run_steps(act, step, {NU * NT - 3: lambda: row_root(0), NU * NT: lambda: [z_out(0, 0), z_out(0, 1)],
                                  NU * NT + 1: lambda: split_hi(0, 0),
                                  NU * NT + 2: lambda: [router_exp(0), split_hi(1, 1)]})
            split_hi(2, 2)
            row_root(1)

            def silu(n, j):
                act.wait_ge(up_done, n + 1)
                ge(act, prod_done, n - 1)
                act.activation(hs[j % 2], ups[j % 2][0][:, :], ACT.Silu, scale=1.0 / WF_SCALE)\
                   .then_inc(silu_done, 1)

            def hidden_hi(n, j):
                act.wait_ge(hid_done, n + 1)
                ge(act, down_done, n - 3)
                act.activation(hh[j], hf[j % 2], ACT.Copy).then_inc(hid_hi, 1)

            def expert(n, j, ahead=True):
                silu(n, j)
                if ahead:
                    split_hi(n + 3, (j + 3) % 4)
                hidden_hi(n, j)

            between = {2: lambda: z_out(1, 0), 4: lambda: z_out(1, 1), 6: lambda: router_exp(1)}
            for n in range(8):
                expert(n, n % 4)
                between.get(n, lambda: None)()
            with act.Fori(2, NX // 2 - 1) as i:
                for j in range(4):
                    expert(4 * i + j, j)
            for j in range(4):
                expert(2 * NX - 4 + j, j, ahead=(j == 0))

        @block.tensor
        def _(pe):
            pe.wait_ge(ld_small, 32)
            for k in range(4):
                half, c = k // HC, k % HC
                pe.wait_ge(xn_done, half + 1)
                for j in range(NHT):
                    t = NHT * half + j
                    mm = pe.transpose(wide_ps[k][:, j * P:(j + 1) * P],
                                      xn[:, t * H + c * P:t * H + c * P + P], idf[:, :])
                mm.then_inc(xT_done, 1)

            def project(t, c, i):
                kind, b = BANKS[4 * c + i]
                n = NU * t + c
                ge(pe, proj_evac, 4 * n + i - 1)
                ps = proj_ps[i % 2][:, :]
                first = isinstance(t, int) and t == 0
                if kind in ("kx", "vx"):
                    if first:
                        pe.wait_ge(ctx_ready, 1)
                        pe.wait_ge(wkv_ready, 1)
                    o = (G * D if kind == "vx" else 0) + 512 * b
                    parts = [(ctxh, wkvh), (ctxh, wkvl), (ctxl, wkvh)]
                    k = 0
                    for a, w in parts:
                        for ch in range(HC):
                            lhs = a[:, ch, bass.ds(t * P, P)]
                            mm = pe.matmul(ps, lhs, w[:, ch, o:o + 512], start=(k == 0), stop=(k == 5))
                            k += 1
                else:
                    j = XORDER.index(kind)
                    pe.wait_ge(xs_ready, t + 1)
                    if first:
                        pe.wait_ge(ld_w[kind], 16)
                    k = 0
                    for a in (XHf, XLf):
                        for ch in range(HC):
                            lhs = a[:, bass.ds(t * XW + (j * HC + ch) * P, P)]
                            mm = pe.matmul(ps, lhs, wb[kind][:, ch, 512 * b:512 * b + 512],
                                           start=(k == 0), stop=(k == 3))
                            k += 1
                mm.then_inc(proj_done, 1)

            def head_transposes(n, c, i):
                pe.wait_ge((norm0_done, norm1_done, norm2_done)[i], n + 1)
                ge(pe, headT_evac, 3 * n + i)
                for h in range(4):
                    if i > 0:
                        dst = headT_ps[:, :].rearrange("p (g b h s) -> p g b h s", g=2, b=2, h=2)\
                            [:, h // 2, :, h % 2, :]
                    else:
                        dst = headT_ps[:, h * P:(h + 1) * P]
                    mm = pe.transpose(dst, raw[c % 2][i][:, h * D:(h + 1) * D], idf[:, :])
                mm.then_inc(headT_done, 1)

            def scores(w, s):
                pe.wait_ge(headT_evac, 3 * w + 3)
                ge(pe, sub_done, w)
                for g in range(4):
                    for b in range(2):
                        mm = pe.matmul(score_ps[:, (2 * g + b) * S:(2 * g + b + 1) * S], qT[:, s, 2 * g + b, :],
                                       kT[:, s, g, b * S:(b + 1) * S], start=True, stop=True)
                mm.then_inc(score_done, 1)

            def prob_transposes(w, s):
                pe.wait_ge(prob_lo, w + 1)
                ge(pe, probT_evac, w)
                ps = probT_ps[:, :].bitcast(F16)
                for g in range(8):
                    mm = pe.transpose(ps[:, g * P:(g + 1) * P], probs[:, s, g * P:(g + 1) * P], idh[:, :])
                mm.then_inc(probT_done, 1)

            def values(w, u):
                pe.wait_ge(probT_evac, w + 1)
                pe.wait_ge(v_lo, w + 1)
                ge(pe, y_done, w)
                pT = probT[u % 2]
                for g in range(4):
                    for b in range(2):
                        rows = slice(b * S, (b + 1) * S)
                        o = pv_ps[b][:, g * P:(g + 1) * P]
                        lo = 512 + g * P
                        vhi, vlo = vh[rows, u, g * D:(g + 1) * D], vl16[rows, u, g * D:(g + 1) * D]
                        pe.matmul(o, vhi, pT[rows, g * P:(g + 1) * P], start=True, stop=False)
                        pe.matmul(o, vhi, pT[rows, lo:lo + P], start=False, stop=False)
                        mm = pe.matmul(o, vlo, pT[rows, g * P:(g + 1) * P], start=False, stop=True)
                mm.then_inc(pv_done, 1)

            def output(w, u, tile):
                pe.wait_ge(catq_done, w + 1)
                if u == 0:
                    ge(pe, res_done, tile)
                for h in range(8):
                    mm = pe.matmul(out_ps[:, 0:H], catq[u % 2][:, h * P:(h + 1) * P], wp[:, 8 * u + h, :],
                                   start=(u == 0 and h == 0), stop=(u == NU - 1 and h == 7))
                mm.then_inc(op_done, 1)

            def z_transposes(half, c):
                pe.wait_ge(xn_done, 3 + half)
                if half == 0 and c == 0:
                    pe.wait_ge(proj_evac, 4 * NU * NT)
                if half == 1 and c == 0:
                    pe.wait_ge(res_done, NT)
                if half == 1:
                    pe.wait_ge(z_evac, HC * half + c)
                for j in range(NHT):
                    mm = pe.transpose(z_ps[half][c][:, j * P:(j + 1) * P],
                                      xn2[half][:, j * H + c * P:j * H + c * P + P], idf[:, :])
                mm.then_inc(z_done, 1)

            def router(half):
                pe.wait_ge(z_evac, HC * (half + 1))
                if half == 0:
                    pe.wait_ge(ld_tail, 32)
                for j in range(NHT):
                    t = NHT * half + j
                    for c in range(HC):
                        mm = pe.matmul(logit_ps[half][:, j * NE:(j + 1) * NE], zT[:, c, t * P:(t + 1) * P],
                                       rws[:, c, :], start=(c == 0), stop=(c == HC - 1))
                mm.then_inc(logit_done, 1)

            def step(t, c):
                n, before = NU * t + c, (c - 1) % NU
                proj, heads, attend = live(n, 0), live(n, 1), live(n, 2)
                if proj:
                    project(t, c, 0)
                if attend:
                    scores(n - 2, c % 2)
                if isinstance(n, int) and n == NU * NT + 1:
                    router(0)
                if proj:
                    project(t, c, 1)
                if live(n, 3):
                    values(n - 3, (c - 3) % NU)
                if live(n, 4) and proj:
                    output(n - 4, c, t - 1)
                if proj:
                    project(t, c, 2)
                if heads:
                    head_transposes(n - 1, before, 0)
                if live(n, 4) and not proj:
                    output(n - 4, c, t - 1)
                if proj:
                    project(t, c, 3)
                if heads:
                    head_transposes(n - 1, before, 1)
                    head_transposes(n - 1, before, 2)
                if attend:
                    prob_transposes(n - 2, c % 2)
                if isinstance(n, int) and n == NU - 1:
                    pe.wait_ge(ld_wp, 16)

            pe.wait_ge(xT_evac, 4)
            pe.wait_ge(idh_done, 1)
            def comb_transposes(half):
                pe.wait_ge(comb_done, half + 1)
                cps = combT_ps[half][:, :].bitcast(BF16)
                for j in range(NHT):
                    mm = pe.transpose(cps[0:NROW, j * P:(j + 1) * P], cbt[:, NHT * half + j, 0:NROW], idb)
                mm.then_inc(combT_done, 1)

            def up(n, e, j, half):
                par = j % 2
                pe.wait_ge(we_lo, n + 1)
                pe.wait_ge(we_hi, n + 1)
                ge(pe, prod_done, n - 1)
                tok = slice(half * 512, half * 512 + 512)
                for wo, ps in ((0, ups[par][0]), (H, ups[par][1])):
                    k = 0
                    for w, z in ((weh[j], zh), (wel[j], zh), (weh[j], zl)):
                        for c in range(HC):
                            mm = pe.matmul(ps[:, :], w[:, wo + c * P:wo + c * P + P], z[:, c, tok],
                                           start=(k == 0), stop=(k == 5))
                            k += 1
                mm.then_inc(up_done, 1)

            def first_up():
                pe.wait_ge(zl_done, 2)
                up(0, 0, 0, 0)

            run_steps(pe, step, {NU * NT: lambda: [z_transposes(0, c) for c in range(HC)],
                                 NU * NT + 3: lambda: [first_up(), comb_transposes(0)]})

            def combine(n, e, half):
                ge(pe, hid_done, n)
                pe.matmul(comb_ps[:, :], sel_sb[:, e, :] if isinstance(e, int)
                          else sel_sb[:, bass.ds(e, 1), :].rearrange("p a m -> p (a m)"),
                          combT[:, half * 512:half * 512 + 512], start=True, stop=True).then_inc(comb_rows, 1)

            def down(n, j, first, last):
                pe.wait_ge(hid_lo, n + 1)
                for i in range(4):
                    ps = pv_ps[i // 2][:, (i % 2) * H:(i % 2) * H + H]
                    ti = slice(i * P, i * P + P)
                    for k, (a, w) in enumerate(((hh, weh), (hl, weh), (hh, wel))):
                        mm = pe.matmul(ps, a[j][:, ti], w[j][:, 2 * H:3 * H],
                                       start=(first and i % 2 == 0 and k == 0), stop=(last and k == 2),
                                       skip_group_check=True)
                mm.then_inc(down_done, 1)

            def expert(n, j):
                m = n + 2
                if m < 2 * NX:
                    up(m, m % NX, m % 4, m // NX)
                if n + 1 < 2 * NX:
                    combine(n + 1, (n + 1) % NX, (n + 1) // NX)
                if n == NX:
                    pe.wait_ge(y_ready, 4)
                down(n, n % 4, n % NX == 0, n % NX == NX - 1)

            pe.wait_ge(combT_evac, 1)
            up(1, 1, 1, 0)
            combine(0, 0, 0)
            between = {2: lambda: z_transposes(1, 0), 4: lambda: z_transposes(1, 1), 5: lambda: router(1)}
            for n in range(8):
                between.get(n, lambda: None)()
                expert(n, n % 4)
            with pe.Fori(2, 4) as i:
                for j in range(4):
                    up(4 * i + j + 2, 4 * i + j + 2, (j + 2) % 4, 0)
                    combine(4 * i + j + 1, 4 * i + j + 1, 0)
                    down(4 * i + j, j, False, False)
            pe.wait_ge(zl_done, 4)
            comb_transposes(1)
            for n in range(16, 20):
                if n == NX - 1:
                    pe.wait_ge(combT_evac, 2)
                expert(n, n % 4)
            with pe.Fori(5, 8) as i:
                for j in range(4):
                    up(4 * i + j + 2, 4 * i + (j + 2 - NX), (j + 2) % 4, 1)
                    combine(4 * i + j + 1, 4 * i + (j + 1 - NX), 1)
                    down(4 * i + j, j, False, False)
            for n in range(32, 36):
                expert(n, n % 4)

        @block.vector
        def _(ve):
            links = [0]

            def link(ins):
                links[0] += 1
                ins.then_inc(dchain, 1)
                ve.wait_ge(dchain, links[0])

            def newton(r, v, a, b):
                link(ve.tensor_tensor(a, v, r, ALU.mult))
                link(ve.tensor_tensor(b, a, r, ALU.mult))
                link(ve.tensor_scalar(a, b, -0.5, 1.5, ALU.mult, ALU.add))
                link(ve.tensor_tensor(r, r, a, ALU.mult))

            def row_stats(t0, t1, loads=None):
                for t in range(t0, t1):
                    if loads and t % NHT == 0:
                        ve.wait_ge(loads[t // NHT], 16)
                    ins = ve.bn_stats(tst[:, t, :], xs[:, t * H:(t + 1) * H])
                link(ins)
                for t in range(t0, t1):
                    ins = ve.bn_aggr(tmv[:, t, :], tst[:, t, :])
                link(ins)

            ve.wait_ge(ld_cols, 16)
            a0, b0 = COL["in_k"][0], COL["in_qx"][1]
            ve.reciprocal(sinv[:, :], colv[:, a0:b0])
            a0, b0 = COL["smooth"]
            ve.reciprocal(smi[:, :], colv[:, a0:b0])
            for x, h0, h1, scale in ((0, 0, 4, "s_k"), (0, 4, NLH, "s_q"), (1, 4, NLH, "s_qx")):
                ve.tensor_copy(lnW[:, x, h0:h1], col(scale).to_broadcast([P, h1 - h0]))
            link(ve.memset(lnW[:, 1, 0:4], 1.0 / WKV_SCALE))
            ve.memset(lnC[:, 2, :, :], EPS)
            ve.memset(lnC[:, 5, :, :], -0.5)
            link(ve.tensor_scalar(lnC[:, 0, :, :], lnW[:, :, :], 1.0 / D, None, ALU.mult))
            link(ve.tensor_tensor(lnC[:, 0, :, :], lnC[:, 0, :, :], lnW[:, :, :], ALU.mult))
            ve.tensor_scalar(lnC[:, 1, :, :], lnC[:, 0, :, :], D / 4.0, None, ALU.mult)
            ve.tensor_scalar(lnC[:, 3, :, :], lnW[:, :, :], -0.5, None, ALU.mult)
            ve.tensor_scalar(lnC[:, 4, :, :], lnW[:, :, :], 1.5, None, ALU.mult).then_inc(prep_done, 1)
            ve.wait_ge(tanh_done, 1)
            ve.tensor_scalar(gate[:, 0:1], th[:, 0:1], col("s_proj"), None, ALU.mult)
            link(ve.tensor_scalar(gate[:, 1:2], th[:, 1:2], 1.0 / WF_SCALE, None, ALU.mult))
            link(ve.tensor_scalar(gate[:, 2:3], gate[:, 0:1], col("s_pin"), None, ALU.mult))

            row_stats(0, NT, ld_x)
            var, mean = tmv[:, :, 1], tmv[:, :, 0]
            ve.tensor_scalar(tw[:, 0, :], var, EPS, None, ALU.add).then_inc(ln_in, 1)
            ve.wait_ge(ln_root, 1)
            newton(tw[:, 2, :], tw[:, 0, :], tw[:, 4, :], tw[:, 5, :])
            link(ve.tensor_copy(tn[:, 0, :], tw[:, 2, :]))
            link(ve.tensor_tensor(tw[:, 4, :], tn[:, 0, :], tn[:, 0, :], ALU.mult))
            link(ve.tensor_tensor(tw[:, 5, :], tw[:, 4, :], var, ALU.mult))
            ve.tensor_scalar(tw[:, 0, :], tw[:, 5, :], EPS, None, ALU.add).then_inc(ln_in, 1)
            ve.wait_ge(ln_root, 2)
            newton(tw[:, 2, :], tw[:, 0, :], tw[:, 4, :], tw[:, 5, :])
            link(ve.tensor_tensor(tn[:, 0, :], tn[:, 0, :], tw[:, 2, :], ALU.mult))
            link(ve.scalar_tensor_tensor(tn[:, 1, :], mean, -1.0, tn[:, 0, :], ALU.mult, ALU.mult))

            for t in range(NT):
                ins = ve.tensor_scalar(xn[:, t * H:(t + 1) * H], xs[:, t * H:(t + 1) * H],
                                       tn[:, 0, t:t + 1], tn[:, 1, t:t + 1], ALU.mult, ALU.add)
                if t % NHT == NHT - 1:
                    ins.then_inc(xn_done, 1)
            ve.wait_ge(ld_small, 32)
            ve.tensor_copy(idh[:, :], idf[:, :]).then_inc(idh_done, 1)

            def to_grid(y, q, sems, n, wait_free=None):
                clip, absolute, mag, big, grid = sems
                ve.tensor_scalar(y, y, FP8_MAX, -FP8_MAX, ALU.min, ALU.max).then_inc(clip, 1)
                ve.wait_ge(clip, n + 1)
                ve.tensor_scalar(ya[:, :].bitcast(U16), y.bitcast(U16), 0x7FFF, None,
                                 ALU.bitwise_and).then_inc(absolute, 1)
                ve.wait_ge(absolute, n + 1)
                ve.tensor_scalar(ym[:, :], ya[:, :], 128.0, 3.0, ALU.mult, ALU.max).then_inc(mag, 1)
                ve.wait_ge(mag, n + 1)
                ve.tensor_tensor(ys[:, :], y, ym[:, :], ALU.add).then_inc(big, 1)
                ve.wait_ge(big, n + 1)
                if wait_free:
                    wait_free()
                ve.tensor_tensor(q, ys[:, :], ym[:, :], ALU.subtract).then_inc(grid, 1)

            def inputs_to_grid(T):
                ve.wait_ge(xin_done, T + 1)
                to_grid(xin[:, :], xin[:, :], (xclip_done, xabs_done, xmag_done, xbig_done, xgrid_done), T)

            in3 = xin[:, :].rearrange("p (j c t) -> p j c t", j=4, c=HC)
            ve.wait_ge(xT_evac, HC)
            ve.tensor_tensor(in3, xT[:, :, 0:P].unsqueeze(1).to_broadcast([P, 4, HC, P]),
                             sinv[:, :].rearrange("p (j c) -> p j c", j=4).unsqueeze(3)
                             .to_broadcast([P, 4, HC, P]), ALU.mult).then_inc(xin_done, 1)
            inputs_to_grid(0)
            ve.wait_ge(xgrid_done, 1)
            a0 = COL["in_k"][0]
            ve.tensor_tensor(xpr[:, :].rearrange("p (n t) -> p n t", t=P),
                             xin[:, :].rearrange("p (n t) -> p n t", t=P),
                             colv[:, a0:a0 + 4 * HC].unsqueeze(2).to_broadcast([P, 4 * HC, P]),
                             ALU.mult).then_inc(xpr_done, 1)
            ve.wait_ge(xhi_done, 1)
            ve.tensor_tensor(XLf[:, 0:XW], xpr[:, :], XHf[:, 0:XW], ALU.subtract).then_inc(xs_ready, 1)

            def stats(n, c, i):
                ve.wait_ge(proj_evac, 4 * n + i + 1)
                for h in range(4):
                    ins = ve.bn_stats(st[:, 4 * i + h, :], raw[c % 2][i][:, h * D:(h + 1) * D])
                if i == 2:
                    ins.then_inc(bn_done, 1)

            def norm_bank1(n, c):
                ve.wait_ge(coef_done, n + 1)
                for h in range(4):
                    r, k = raw[c % 2][1][:, h * D:(h + 1) * D], 4 + h
                    ins = ve.tensor_scalar(r, r, cw[:, k:k + 1], cb[:, k:k + 1], ALU.mult, ALU.add)
                ins.then_inc(norm1_done, 1)

            def softmax_in(w, s):
                s3 = score_ps[:, :].rearrange("p (g t) -> p g t", t=S)
                ve.wait_ge(score_done, w + 1)
                ve.tensor_reduce(mx[:, :], s3, AX.X, ALU.max).then_inc(max_done, 1)
                ve.wait_ge(max_done, w + 1)
                ge(ve, probn_done, w - 1)
                ve.tensor_tensor(prob[s].rearrange("p (g t) -> p g t", t=S), s3,
                                 mx[:, :].unsqueeze(2).to_broadcast([P, 8, S]),
                                 ALU.subtract).then_inc(sub_done, 1)

            def softmax_sum(w, s):
                ve.wait_ge(exp_done, w + 1)
                ve.tensor_reduce(sm[:, :], prob[s].rearrange("p (g t) -> p g t", t=S), AX.X,
                                 ALU.add).then_inc(sum_done, 1)
                ve.wait_ge(sum_done, w + 1)
                ve.reciprocal(rinv[:, s, :], sm[:, :]).then_inc(rinv_done, 1)

            def over_smooth(w, u):
                ve.wait_ge(pv_done, w + 1)
                y3 = yv[:, :].rearrange("p (h t) -> p h t", t=P)
                for b in range(2):
                    ins = ve.tensor_tensor(y3[:, :, b * S:(b + 1) * S],
                                           pv_ps[b][:, :].rearrange("p (h t) -> p h t", t=S),
                                           smi[:, 8 * u:8 * u + 8].unsqueeze(2).to_broadcast([P, 8, S]),
                                           ALU.mult)
                ins.then_inc(y_done, 1)

            def quantise(w, u):
                ve.wait_ge(y_done, w + 1)
                to_grid(yv[:, :], catq[u % 2], (clip_done, abs_done, mag_done, big_done, catq_done), w,
                        lambda: ge(ve, op_done, w - 1))

            def residual(t):
                ve.wait_ge(op_done, NU * (t + 1))
                xt = xs[:, bass.ds(t * H, H)]
                ve.scalar_tensor_tensor(xt, out_ps[:, 0:H], gate[:, 2:3], xt, ALU.mult, ALU.add)\
                  .then_inc(res_done, 1)

            def step(t, c):
                n, before = NU * t + c, (c - 1) % NU
                proj, heads, attend = live(n, 0), live(n, 1), live(n, 2)
                if attend:
                    softmax_in(n - 2, c % 2)
                if heads:
                    norm_bank1(n - 1, before)
                if attend:
                    softmax_sum(n - 2, c % 2)
                if live(n, 3):
                    over_smooth(n - 3, (c - 3) % NU)
                if proj:
                    stats(n, c, 0)
                    stats(n, c, 1)
                    stats(n, c, 2)
                if live(n, 3):
                    quantise(n - 3, (c - 3) % NU)
                if proj and c == 1 and live(n, -NU):
                    inputs_to_grid(t + 1)
                if c == 3 and live(n, NU):
                    residual(t - 1)
                if isinstance(n, int) and n == 0:
                    ve.wait_ge(ld_ctx, 16)
                    ve.tensor_copy(ctxh[:, :, :].rearrange("p c t -> p (c t)"), ctx_st).then_inc(ctx_hi, 1)
                if isinstance(n, int) and n == 1:
                    ve.wait_ge(wkv_hi, 1)
                    ve.scalar_tensor_tensor(wkvl[:, :, :].rearrange("p c t -> p (c t)"), wkv_st, WKV_SCALE,
                                            wkvh[:, :, :].rearrange("p c t -> p (c t)"), ALU.mult,
                                            ALU.subtract).then_inc(wkv_ready, 1)

            def rows_in(half):
                r = slice(NHT * half, NHT * half + NHT)
                ve.wait_ge(res_done, NHT * (half + 1))
                row_stats(r.start, r.stop)
                ve.tensor_scalar(tw[:, 0, r], var[:, r], EPS, None, ALU.add).then_inc(ln_in, 1)

            def rows_scale(half):
                r = slice(NHT * half, NHT * half + NHT)
                ve.wait_ge(ln_root, 3 + half)
                newton(tw[:, 2, r], tw[:, 0, r], tw[:, 4, r], tw[:, 5, r])
                link(ve.scalar_tensor_tensor(tn[:, 1, r], mean[:, r], -1.0, tw[:, 2, r], ALU.mult, ALU.mult))

            def rows_out(half):
                if half == 0:
                    ve.wait_ge(xs_ready, NT)
                for j in range(NHT):
                    t = NHT * half + j
                    ins = ve.tensor_scalar(xn2[half][:, j * H:(j + 1) * H], xs[:, t * H:(t + 1) * H],
                                           tw[:, 2, t:t + 1], tn[:, 1, t:t + 1], ALU.mult, ALU.add)
                ins.then_inc(xn_done, 1)

            def z_low(half, c):
                sl = slice(half * 512, half * 512 + 512)
                ve.wait_ge(z_evac, HC * half + c + 1)
                ve.tensor_tensor(zl[:, c, sl], zT[:, c, sl], zh[:, c, sl], ALU.subtract).then_inc(zl_done, 1)

            def z_low0(half):
                z_low(half, 0)

            def z_low1(half):
                z_low(half, 1)

            iota = rowv[:, NE:2 * NE].unsqueeze(1).to_broadcast([P, NHT, NE])

            def over_experts(a):
                return a.unsqueeze(2).to_broadcast([P, NHT, NE])

            def route_top(half):
                r = slice(NHT * half, NHT * half + NHT)
                logits, biased, ex = [a[:, r, :] for a in rt[:3]]
                ve.wait_ge(logit_done, half + 1)
                link(ve.tensor_copy(logits, logit_ps[half][:, 0:NHT * NE].rearrange("p (t e) -> p t e", t=NHT)))
                ve.tensor_tensor(biased, logits, rowv[:, 0:NE].unsqueeze(1).to_broadcast([P, NHT, NE]), ALU.add)
                link(ve.tensor_reduce(rs8[:, 0, r], logits, AX.X, ALU.max))
                ve.tensor_tensor(ex, logits, over_experts(rs8[:, 0, r]), ALU.subtract).then_inc(rexp_in, 1)
                for t in range(r.start, r.stop):
                    ins = ve.max(m8[:, t, :], rt[1][:, t, :])
                link(ins)

            def route_mask(half):
                r = slice(NHT * half, NHT * half + NHT)
                m1, m2 = rt[3][:, r, :], rt[4][:, r, :]
                for t in range(r.start, r.stop):
                    ins = ve.max_index(i8[:, t, :], m8[:, t, :], rt[1][:, t, :])
                link(ins)
                link(ve.tensor_copy(i8f[:, r, :], i8[:, r, :]))
                ve.tensor_tensor(m1, iota, i8f[:, r, 0:1].to_broadcast([P, NHT, NE]), ALU.is_equal)
                link(ve.tensor_tensor(m2, iota, i8f[:, r, 1:2].to_broadcast([P, NHT, NE]), ALU.is_equal))
                link(ve.tensor_tensor(m1, m1, m2, ALU.add))

            def route_weights(half):
                r = slice(NHT * half, NHT * half + NHT)
                ex, m1, m2, comb, rem, rem2 = [a[:, r, :] for a in rt[2:8]]
                c16 = cbt[:, r, :]
                ve.wait_ge(rexp_done, half + 1)
                link(ve.tensor_tensor(m2, ex, m1, ALU.mult))
                link(ve.tensor_reduce(rs8[:, 1, r], m2, AX.X, ALU.add))
                link(ve.reciprocal(rs8[:, 2, r], rs8[:, 1, r]))
                link(ve.tensor_tensor(comb, m2, over_experts(rs8[:, 2, r]), ALU.mult))
                link(ve.tensor_copy(c16[:, :, 0:NE], comb))
                link(ve.tensor_tensor(rem, comb, c16[:, :, 0:NE], ALU.subtract))
                link(ve.tensor_copy(c16[:, :, NE:2 * NE], rem))
                link(ve.tensor_tensor(rem2, rem, c16[:, :, NE:2 * NE], ALU.subtract))
                link(ve.tensor_copy(c16[:, :, 2 * NE:3 * NE], rem2))
                ve.memset(c16[:, :, 3 * NE:4 * NE], 1.0).then_inc(comb_done, 1)

            def weights_out(half):
                ve.wait_ge(combT_done, half + 1)
                ve.tensor_copy(combT[:, half * 512:half * 512 + 512],
                               combT_ps[half][:, :].bitcast(BF16)[0:NROW, 0:512]).then_inc(combT_evac, 1)

            def in_turn(half, *parts):
                def run():
                    for part in parts:
                        part(half)
                return run

            last = NU * NT
            def split_lo(n, j):
                ve.wait_ge(we_hi, n + 1)
                ve.scalar_tensor_tensor(wel[j], wst[j % 2], WF_SCALE, weh[j], ALU.mult,
                                        ALU.subtract).then_inc(we_lo, 1)

            def first_low(n):
                return lambda half: split_lo(n, n)

            def identity16(half):
                link(ve.tensor_copy(idb, idf[:, :]))

            run_steps(ve, step, {
                last - 3: in_turn(0, rows_in), last - 2: in_turn(0, rows_scale, rows_out),
                last + 1: in_turn(0, z_low0, z_low1),
                last + 2: in_turn(0, route_top, route_mask, first_low(0), identity16, route_weights),
                last + 3: in_turn(0, first_low(1), weights_out)})
            rows_in(1)
            split_lo(2, 2)

            def hidden(n, j):
                par = j % 2
                ve.wait_ge(silu_done, n + 1)
                ve.scalar_tensor_tensor(ht[par], ups[par][1][:, :], 1.0 / WF_SCALE, hs[par], ALU.mult,
                                        ALU.mult).then_inc(prod_done, 1)
                ve.wait_ge(prod_done, n + 1)
                ve.wait_ge(comb_rows, n + 1)
                ge(ve, hid_lo, n - 1)
                ge(ve, hid_hi, n - 1)
                ve.tensor_tensor(hf[par], ht[par], comb_ps[:, :], ALU.mult).then_inc(hid_done, 1)

            def results(half):
                ve.wait_ge(down_done, NX * (half + 1))
                for j in range(4):
                    t = 4 * half + j
                    ve.scalar_tensor_tensor(yo[t], pv_ps[j // 2][:, (j % 2) * H:(j % 2) * H + H],
                                            gate[:, 1:2], xs[:, t * H:(t + 1) * H], ALU.mult,
                                            ALU.add).then_inc(y_ready, 1)

            def expert(n, j, ahead=True):
                hidden(n, j)
                if ahead:
                    split_lo(n + 3, (j + 3) % 4)

            between = {0: in_turn(1, rows_scale), 1: in_turn(1, rows_out), 3: in_turn(1, z_low0), 4: in_turn(1, z_low1),
                       5: in_turn(1, route_top), 6: in_turn(1, route_mask), 7: in_turn(1, route_weights)}
            for n in range(8):
                expert(n, n % 4)
                between.get(n, lambda: None)()
            with ve.Fori(2, 4) as i:
                for j in range(4):
                    expert(4 * i + j, j)
            weights_out(1)
            for n in range(16, 20):
                if n == NX + 1:
                    results(0)
                expert(n, n % 4)
            with ve.Fori(5, 8) as i:
                for j in range(4):
                    expert(4 * i + j, j)
            for n in range(32, 36):
                expert(n, n % 4, ahead=(n == 32))
            results(1)


def kernel(**inputs):
    import concourse.bacc as bacc
    from concourse.bass_utils import run_bass_kernel_spmd as run

    v = {k: np.asarray(a) for k, a in inputs.items()}
    at = {k[len("L0_xattn_"):]: a for k, a in v.items() if k.startswith("L0_xattn_")}
    ff = {k[len("L0_ffn_"):]: a for k, a in v.items() if k.startswith("L0_ffn_")}

    def per_row(a):
        return np.ascontiguousarray(a.reshape(-1, P).T)

    def everywhere(a):
        return np.broadcast_to(a.reshape(1, 1), (P, 1))

    cols = np.concatenate(
        [per_row(at[k]) for k in ("ln_w", "ln_b", "k_in_scale", "q_in_scale", "v_in_scale", "qx_in_scale",
                                  "qln_w", "kln_w", "qxln_w", "kxln_w", "qln_b", "kln_b", "qxln_b", "kxln_b",
                                  "proj_smooth")]
        + [everywhere(a) for a in (at["wq_scale"], at["wk_scale"], at["wqx_scale"], at["wv_scale"],
                                   at["proj_w_scale"], at["proj_in_scale"], v["g_xattn"], v["g_ffn"])], axis=1)
    rowc = np.concatenate([np.broadcast_to(ff["router_bias"][None, :], (P, NE)),
                           np.broadcast_to(np.arange(NE, dtype=np.float32)[None, :], (P, NE))], axis=1)
    sel = np.zeros((NROW, NX, P), np.float32)
    for e in range(NX):
        for r in ((e, NE + e, 2 * NE + e) if e < NE else (3 * NE,)):
            sel[r, e, :] = 1.0

    def up(we, ws):
        a = np.concatenate([we.transpose(1, 0, 2).reshape(H, NE * FE), ws[0]], axis=1)
        return a.reshape(HC, P, NX, FE).transpose(2, 1, 0, 3).reshape(NX, P, HC * FE)

    wffn = np.concatenate([up(ff["Wu"], ff["Su"]), up(ff["Wg"], ff["Sg"]),
                           np.concatenate([ff["Wd"], ff["Sd"][0].reshape(NSH, FE, H)], axis=0)], axis=2)
    arrays = {
        "x": v["x"].reshape(TOK, H), "cols": cols, "rowc": rowc, "ident": np.eye(P, dtype=np.float32),
        "sel": sel.reshape(NROW, NX * P), "ctxT": v["ctx_2048"].reshape(TOK, H).T,
        "wkvT": at["w_kv_x"].T, "wqT": at["wq"].T, "wkT": at["wk"].T, "wvT": at["wv"].T,
        "wqxT": at["wqx"].T, "wpT": at["wproj"].T, "rwT": ff["router_w"].T, "wffn": wffn,
    }
    nc = bacc.Bacc("TRN2", target_bir_lowering=False, num_devices=1)
    feed, args = {}, []
    for name, a in arrays.items():
        a = np.ascontiguousarray(a)
        feed["in_" + name] = a
        args.append(nc.dram_tensor("in_" + name, a.shape, mybir.dt.from_np(a.dtype), kind="ExternalInput").ap())
    args.append(nc.dram_tensor("out_y", (TOK, H), F32, kind="ExternalOutput").ap())
    build(nc, *args)
    r = run(nc, [feed], core_ids=[0])
    return r.results[0]["out_y"].reshape(NB, S, H)
```
